# Optimizing a Trainium2 kernel written in Bass

```python
import numpy as np
import jax
import jax.numpy as jnp

def _softmax(x, axis=-1):
    return jax.nn.softmax(x, axis=axis)

def _gelu(x):
    return jax.nn.gelu(x, approximate=True)

def _silu(x):
    return jax.nn.silu(x)

def _sigmoid(x):
    return jax.nn.sigmoid(x)

def _layernorm(x, axis=-1, eps=1e-05):
    m = jnp.mean(x, axis=axis, keepdims=True)
    v = jnp.var(x, axis=axis, keepdims=True)
    return (x - m) / jnp.sqrt(v + eps)

def _scatter_add(tgt, idx, src, axis=0):
    return tgt.at[idx].add(src)

def _segment_sum(src, seg, n):
    return jax.ops.segment_sum(src, seg, n)
kernel_name = 'mk_macaron_d1_jaxref_r2_fcdcc5'

def setup_inputs(seed: int=0):
    np.random.seed(seed)
    _w = jnp.asarray

    def _L0_attn_setup():
        import jax, jax.numpy as jnp
        import numpy as np
        import math
        B, T, D, H = (2, 1024, 512, 16)
        DH = D // H

        def _rope_tensor(t, dh):
            pos = jnp.arange(t, dtype=jnp.float32)
            angles = pos[:, None] / 10000.0 ** (jnp.arange(0, dh, 2, dtype=jnp.float32) / dh)
            rope = jnp.stack([jnp.cos(angles), jnp.sin(angles)], axis=-1).reshape(t, dh)
            return rope

        def _rotate(x):
            return jnp.stack([-x[..., 1::2], x[..., 0::2]], axis=-1).reshape(x.shape)
        key = jax.random.key(seed)
        k1, k2, k3 = jax.random.split(key, 3)
        x = jax.random.normal(k1, (B, T, D), dtype=jnp.float32)
        Wqkv = jax.random.normal(k2, (3 * D, D), dtype=jnp.float32) * 0.02
        bqkv = jnp.zeros((3 * D,), dtype=jnp.float32)
        Wproj = jax.random.normal(k3, (D, D), dtype=jnp.float32) * 0.02
        bproj = jnp.zeros((D,), dtype=jnp.float32)
        return {'x': x, 'Wqkv': Wqkv, 'bqkv': bqkv, 'Wproj': Wproj, 'bproj': bproj}
    _L0_attn_in = _L0_attn_setup()

    def _L0_ffn_setup():
        import jax, jax.numpy as jnp
        import numpy as np
        D_MODEL = 512
        M = 64
        INNER = 16
        key = jax.random.key(seed)
        ks = jax.random.split(key, 9)

        def init(k, shape, fan_in):
            bound = 1.0 / np.sqrt(fan_in)
            return jax.random.uniform(k, shape, jnp.float32, -bound, bound)
        x = jax.random.normal(ks[0], (16, 2048, D_MODEL), dtype=jnp.float32)
        Win = init(ks[1], (D_MODEL, M), D_MODEL)
        bin_ = init(ks[2], (M,), D_MODEL)
        W1 = init(ks[3], (M, INNER), 1)
        b1 = init(ks[4], (M, INNER), 1)
        W2 = init(ks[5], (M, INNER), INNER)
        b2 = init(ks[6], (M,), INNER)
        Wout = init(ks[7], (M, D_MODEL), M)
        bout = init(ks[8], (D_MODEL,), M)
        return {'x': x, 'Win': Win, 'bin_': bin_, 'W1': W1, 'b1': b1, 'W2': W2, 'b2': b2, 'Wout': Wout, 'bout': bout}
    _L0_ffn_in = _L0_ffn_setup()
    _d = {'L0_attn_x': _L0_attn_in['x'], 'L0_attn_Wqkv': _L0_attn_in['Wqkv'], 'L0_attn_bqkv': _L0_attn_in['bqkv'], 'L0_attn_Wproj': _L0_attn_in['Wproj'], 'L0_attn_bproj': _L0_attn_in['bproj'], 'L0_ffn_Win': _L0_ffn_in['Win'], 'L0_ffn_bin_': _L0_ffn_in['bin_'], 'L0_ffn_W1': _L0_ffn_in['W1'], 'L0_ffn_b1': _L0_ffn_in['b1'], 'L0_ffn_W2': _L0_ffn_in['W2'], 'L0_ffn_b2': _L0_ffn_in['b2'], 'L0_ffn_Wout': _L0_ffn_in['Wout'], 'L0_ffn_bout': _L0_ffn_in['bout']}
    _x0 = _d['L0_attn_x']
    _d['L0_attn_x'] = jax.random.normal(jax.random.fold_in(jax.random.key(seed), 1), (4, 2048, 512), dtype=_x0.dtype)
    del _x0
    return _d

def reference(L0_attn_x, L0_attn_Wqkv, L0_attn_bqkv, L0_attn_Wproj, L0_attn_bproj, L0_ffn_Win, L0_ffn_bin_, L0_ffn_W1, L0_ffn_b1, L0_ffn_W2, L0_ffn_b2, L0_ffn_Wout, L0_ffn_bout):

    def _L0_attn_ref(x, Wqkv, bqkv, Wproj, bproj):
        import jax, jax.numpy as jnp
        import numpy as np
        import math
        B, T, D, H = (2, 1024, 512, 16)
        DH = D // H

        def _rope_tensor(t, dh):
            pos = jnp.arange(t, dtype=jnp.float32)
            angles = pos[:, None] / 10000.0 ** (jnp.arange(0, dh, 2, dtype=jnp.float32) / dh)
            rope = jnp.stack([jnp.cos(angles), jnp.sin(angles)], axis=-1).reshape(t, dh)
            return rope

        def _rotate(x):
            return jnp.stack([-x[..., 1::2], x[..., 0::2]], axis=-1).reshape(x.shape)
        b, t, d = x.shape
        qkv = x @ Wqkv.T + bqkv
        qkv = qkv.reshape(b, t, H, 3 * DH).transpose(0, 2, 1, 3)
        q, k, v = jnp.split(qkv, 3, axis=-1)
        rope = _rope_tensor(t, DH)
        q = q * rope + _rotate(q) * (1.0 - rope)
        k = k * rope + _rotate(k) * (1.0 - rope)
        att = jnp.einsum('bhtd,bhsd->bhts', q, k) * (1.0 / math.sqrt(DH))
        causal = jnp.tril(jnp.ones((t, t), dtype=bool))
        att = jnp.where(causal, att, -jnp.inf)
        att = jax.nn.softmax(att, axis=-1)
        y = jnp.einsum('bhts,bhsd->bhtd', att, v)
        y = y.transpose(0, 2, 1, 3).reshape(b, t, d)
        return y @ Wproj.T + bproj

    def _L0_ffn_ref(x, Win, bin_, W1, b1, W2, b2, Wout, bout):
        import jax, jax.numpy as jnp
        import numpy as np
        D_MODEL = 512
        M = 64
        INNER = 16
        s = jnp.einsum('btd,dm->btm', x, Win) + bin_
        h = jax.nn.relu(s[..., None] * W1 + b1)
        g = jnp.einsum('btmh,mh->btm', h, W2) + b2
        out = jnp.einsum('btm,md->btd', g, Wout) + bout
        return out
    x = L0_attn_x
    x = x + 0.5 * _L0_ffn_ref(_layernorm(x, axis=-1), L0_ffn_Win, L0_ffn_bin_, L0_ffn_W1, L0_ffn_b1, L0_ffn_W2, L0_ffn_b2, L0_ffn_Wout, L0_ffn_bout)
    x = x + _L0_attn_ref(_layernorm(x, axis=-1), L0_attn_Wqkv, L0_attn_bqkv, L0_attn_Wproj, L0_attn_bproj)
    x = x + 0.5 * _L0_ffn_ref(_layernorm(x, axis=-1), L0_ffn_Win, L0_ffn_bin_, L0_ffn_W1, L0_ffn_b1, L0_ffn_W2, L0_ffn_b2, L0_ffn_Wout, L0_ffn_bout)
    return x

_drawn_inputs = setup_inputs


def setup_inputs(seed=0):
    import zlib

    import numpy as np

    out = dict(_drawn_inputs(seed))
    spreads = {'L0_attn_bqkv': (0.0, 0.1), 'L0_attn_bproj': (0.0, 0.1)}
    factors = {'L0_ffn_bin_': 8.0}
    for name, (base, spread) in spreads.items():
        noise = np.random.default_rng([zlib.crc32(name.encode()), seed]).standard_normal(out[name].shape)
        drawn = base * np.exp(spread * noise) if base else spread * noise
        out[name] = jnp.asarray(drawn.astype(out[name].dtype))
    for name, factor in factors.items():
        out[name] = (out[name] * factor).astype(out[name].dtype)
    return out
```

```python
from contextlib import ExitStack

import numpy as np

import concourse.bass as bass
from concourse import mybir

F32 = mybir.dt.float32
F32R = mybir.dt.float32r
BF16 = mybir.dt.bfloat16
ALU = mybir.AluOpType
ACT = mybir.ActivationFunctionType
AX_X = mybir.AxisListType.X

P = 128
B, S, D, H = 4, 2048, 512, 16
DH = D // H
TOK = B * S
M, INNER = 64, 16
KC = D // P
GT = 4
GTOK = GT * P
NG = TOK // GTOK
GB = S // GTOK
HG = 4
NHG = H // HG
NE = M * INNER // P
EPS = 1e-5
MASK = -3.0e38


SPLITS = ((0, 0), (0, 1), (1, 0))
T_BANKS = F_BANKS = Q_BANKS = R_BANKS = 2
STAT_TICKS = 3 * GT
NORM_TICKS = STAT_TICKS + 5


def order_first():
    q = [("qkv", j, n) for j in range(GT) for n in range(3)]
    rope = [("rope", j) for j in range(GT)]
    r = [("turn_qk", c) for c in range(2 * KC)]
    t = [[("turn", n, kc) for kc in range(KC)] for n in range(2)]
    e = [("hidden", j) for j in range(NE)]
    o = [("ffn", j) for j in range(GT)]
    return (r[0:3] + q[0:1] + [("stats", 0)] + r[3:6] + q[1:2] + [("norm", 0)] + r[6:8] + q[2:3] + rope[0:1] + q[3:4]
            + t[0][0:2] + q[4:5] + t[0][2:4] + q[5:6] + rope[1:2] + [("s",)] + q[6:7] + e[0:4] + q[7:8] + e[4:8]
            + q[8:9] + rope[2:3] + [("inner",)] + q[9:10] + o + [("stats", 1)] + q[10:11] + [("norm", 1)] + q[11:12]
            + rope[3:4] + t[1])


def order_last():
    p = [("proj", j) for j in range(GT)]
    t = [("turn", 0, kc) for kc in range(KC)]
    e = [("hidden", j) for j in range(NE)]
    o = [("ffn", j) for j in range(GT)]
    return ([("split",), ("s",)] + e[0:2] + p[0:1] + e[2:4] + p[1:2] + e[4:6] + p[2:3] + e[6:8] + p[3:4]
            + [("stats", 0), ("inner",)] + o[0:2] + [("norm", 0)] + o[2:4] + t)


def dense(nc, first, w, x_in_all, x_out_all, yt_all, qk_t, v_all):
    order = order_first() if first else order_last()
    name = "f_" if first else "l_"
    ffn_kinds = ("s", "hidden", "inner", "ffn")
    if first:
        offset = {k: 1 for k in ("stats", "norm", "turn") + ffn_kinds}
        offset.update(qkv=0, rope=0, turn_qk=-1)
    else:
        offset = {k: 1 for k in ("split", "proj", "stats", "norm", "turn")}
        offset.update({k: 0 for k in ffn_kinds})
    norms = sum(x[0] == "stats" for x in order)
    t_uses = [x for x in order if x[0] in ("proj", "turn")]
    f_uses = [x for x in order if x[0] in ffn_kinds]
    q_uses = [x for x in order if x[0] == "qkv"]
    f_owner = ["dve" if x[0] in ("s", "ffn") else "act" for x in f_uses]

    with ExitStack() as ctx:
        def sb(n, shape, dt=F32):
            return ctx.enter_context(nc.sbuf_tensor(name + n, shape, dt))

        def psum(n):
            return ctx.enter_context(nc.psum_tensor(name + n, [P, 2, GTOK], F32))

        def sem(n):
            return ctx.enter_context(nc.semaphore(name + n))

        ident = sb("ident", [P, P])
        sel = sb("sel", [P, NE, P], F32R)
        win = sb("win", [P, 2, KC, P], F32R)
        b_in = sb("b_in", [P, 1])
        w1 = sb("w1", [P, NE])
        b1 = sb("b1", [P, NE])
        w2 = sb("w2", [P, NE, DH])
        b2 = sb("b2", [P, 1])
        w_out = sb("w_out", [P, D])
        x_sb = sb("x_sb", [P, 2, GT, D])
        xn = sb("xn", [P, GT, D])
        stats = sb("stats", [P, GT, 6])
        mean_var = sb("mean_var", [P, GT, 2])
        var_eps = sb("var_eps", [P, GT])
        std = sb("std", [P, GT])
        rstd = sb("rstd", [P, 4, GT])
        n_xt = 2 if first else 1
        xt = sb("xt", [P, n_xt, 2, KC, GTOK], F32R)
        s_parts = sb("s_parts", [P, GTOK], F32R)
        hid = sb("hid", [P, NE, GTOK])
        inner = sb("inner", [P, GTOK])
        cols = 3 * D if first else D
        w_mm = sb("w_mm", [P, 2, KC, cols], F32R)
        bias = sb("bias", [P, cols])
        if first:
            qkv = sb("qkv", [P, GT, 3 * D])
            stage = qkv
            turned_in = sb("turned_in", [P, GT, 2 * D])
            products = sb("products", [P, 2, 2 * D])
            staged = products
            rope = sb("rope", [P, 2, GT, 2, 2, DH])
            qk_parts = sb("qk_parts", [P, 2, 2, GTOK], F32R)
        else:
            stage = sb("stage", [P, KC, D])
            staged = sb("staged", [P, 2, 2 * D])
            y_sb = sb("y_sb", [P, 2, KC, GTOK])
            y_parts = sb("y_parts", [P, 2, KC, GTOK], F32R)

        sel32 = staged[:, 0, :].rearrange("p (e q) -> p e q", e=NE)
        win32 = staged[:, 1, 0:KC * P].rearrange("p (k m) -> p k m", k=KC)

        ps_t, ps_f = psum("ps_t"), psum("ps_f")
        if first:
            ps_q, ps_r = psum("ps_q"), psum("ps_r")

        weights_in = sem("weights_in")
        weights_set = sem("weights_set")
        x_in = [sem("x_in0"), sem("x_in1")]
        x_out = [sem("x_out0"), sem("x_out1")]
        ticks = sem("ticks")
        std_done = sem("std_done")
        xn_done = sem("xn_done")
        t_done = sem("t_done")
        t_first = sem("t_first")
        t_free = sem("t_free")
        f_done = sem("f_done")
        s_first = sem("s_first")
        f_free = {"dve": sem("f_free_dve"), "act": sem("f_free_act")}
        if first:
            rope_in = [sem("rope_in0"), sem("rope_in1")]
            v_out = sem("v_out")
            q_done = sem("q_done")
            q_free = sem("q_free")
            rope_mul = sem("rope_mul")
            rope_done = sem("rope_done")
            r_done = sem("r_done")
            r_first = sem("r_first")
            r_free = sem("r_free")
            qk_out = [sem("qk_out0"), sem("qk_out1")]
        else:
            y_in = [sem("y_in0"), sem("y_in1")]
            y_first = sem("y_first")
            y_split = sem("y_split")
            x_biased = sem("x_biased")

        n_f = len(f_uses)
        f_per = {e: f_owner.count(e) for e in f_free}
        f_nth = [f_owner[:i + 1].count(f_owner[i]) for i in range(n_f)]
        SLOT_CREDIT, F_DONE_CREDIT, Q_DONE_CREDIT, T_DONE_CREDIT = 2, 16, 1, 8
        V_OUT_CREDIT, QK_OUT_CREDIT, N_LOADS = 16, 32, 12

        def wait_f_bank(eng, g, n):
            m = n - F_BANKS
            owner = f_owner[m]
            nth = f_nth[m] - (f_per[owner] if m < 0 else 0)
            eng.wait_ge(f_free[owner], g * f_per[owner] + (SLOT_CREDIT + nth))

        def wait_f_taken(eng, g, use):
            n = f_uses.index(use)
            eng.wait_ge(f_free[f_owner[n]], g * f_per[f_owner[n]] + (SLOT_CREDIT + f_nth[n]))

        low, high = -max(offset.values()), NG - min(offset.values())
        mid_low, mid_high = -min(offset.values()), NG - 2 - offset["ffn"]
        pairs = (mid_high - mid_low) // 2

        def schedule(eng, step):
            for c in range(low, mid_low):
                step(0, c)
            with eng.Fori(0, pairs) as i:
                step(i, mid_low)
                step(i, mid_low + 1)
            for c in range(mid_low + 2 * pairs, high):
                step(0, c)

        def at(kind, i, c):
            c += offset[kind]
            if isinstance(i, int) and not 0 <= c < NG:
                return None
            return i * 2 + c, i + c // 2, c % 2

        with nc.Block() as block:

            @block.sync
            def _(sp):
                loads = [(ident[:, :], w["ident"]), (sel32[:, :, :], w["sel"]),
                         (win32[:, :, 0:M], w["w_in"].rearrange("(k p) m -> p k m", p=P)),
                         (win32[:, :, M:P], w["w_in"].rearrange("(k p) m -> p k m", p=P)),
                         (b_in[:, :], w["b_in"]), (w1[:, :], w["w1"]), (b1[:, :], w["b1"]),
                         (w2[:, :, :], w["w2"]), (b2[:, :], w["b2"]), (w_out[:, :], w["w_out"]),
                         (bias[:, :], (w["b_qkv"] if first else w["b_proj"]).partition_broadcast(P)),
                         (stage[:, :, :], (w["w_qkv"] if first else w["w_proj"]).rearrange("(k p) n -> p k n", p=P))]
                for dst, src in loads:
                    sp.dma_start(dst, src).then_inc(weights_in, 16)
                assert len(loads) == N_LOADS

                def tokens(g):
                    return bass.ds(g * GTOK, GTOK)

                def load_x(g, slot):
                    sp.dma_start(x_sb[:, slot, :, :], x_in_all[tokens(g), :].rearrange("(j p) d -> p j d", p=P))\
                      .then_inc(x_in[slot], 16)
                    if not first:
                        sp.dma_start(y_sb[:, slot, :, :], yt_all[bass.ds(g, 1), :, :, :].rearrange(
                            "o h p s -> p (o h) s")).then_inc(y_in[slot], 16)

                def load_rope(g, slot):
                    sp.dma_start(rope[:, slot, :, :, :, :].rearrange("p j a b d -> p j (a b d)"),
                                 w["rope"][tokens(g), :].rearrange("(j p) c -> p j c", p=P)).then_inc(rope_in[slot], 16)

                for g in range(2):
                    load_x(g, g)
                    if first:
                        load_rope(g, g)

                def step(i, c):
                    last = isinstance(i, int)
                    if first and at("turn_qk", i, c):
                        g, _, _ = at("turn_qk", i, c)
                        at_tokens = bass.ds(i * (2 * GTOK) + GTOK * (c + offset["turn_qk"]), GTOK)
                        for h in range(2 * KC):
                            sp.wait_ge(r_free, g * (2 * KC) + (R_BANKS + h + 1))
                            for part in range(2):
                                sp.dma_start(qk_t[h, part, :, at_tokens], qk_parts[:, h % 2, part, :].bitcast(F32))\
                                  .then_inc(qk_out[h % 2], 16)
                    if first and at("qkv", i, c):
                        g, _, slot = at("qkv", i, c)
                        sp.wait_ge(q_free, g * (3 * GT) + (Q_BANKS + 3 * GT))
                        sp.dma_start(v_all[tokens(g), :].rearrange("(j p) d -> p j d", p=P),
                                     qkv[:, :, 2 * D:3 * D]).then_inc(v_out, 16)
                        if not last or g + 2 < NG:
                            sp.wait_ge(rope_mul, g * (4 * GT) + 4 * GT)
                            load_rope(g + 2, slot)
                    if at("ffn", i, c):
                        g, half, slot = at("ffn", i, c)
                        wait_f_taken(sp, g, ("ffn", GT - 1))
                        sp.dma_start(x_out_all[tokens(g), :].rearrange("(j p) d -> p j d", p=P), x_sb[:, slot, :, :])\
                          .then_inc(x_out[slot], 16)
                        if not last or g + 2 < NG:
                            sp.wait_ge(x_out[slot], half * 16 + 16)
                            if first:
                                sp.wait_ge(xn_done, g * (norms * GT) + norms * GT)
                            load_x(g + 2, slot)

                schedule(sp, step)
                for slot in range(2):
                    sp.wait_ge(x_out[slot], 16 * (NG // 2))
                    if first:
                        sp.wait_ge(qk_out[slot], QK_OUT_CREDIT + NG * KC * 32)
                if first:
                    sp.wait_ge(v_out, V_OUT_CREDIT + 16 * NG)

            @block.gpsimd
            def _(pool):
                def rotate(i, c, j):
                    g, half, slot = at("rope", i, c)
                    if j == 0:
                        pool.wait_ge(rope_in[slot], half * 16 + 16)
                    pool.wait_ge(q_free, g * (3 * GT) + (Q_BANKS + 3 * j + 2))
                    pool.wait_ge(rope_done, g * GT + (1 + j))
                    for n in range(2):
                        src = qkv[:, j, n * D:n * D + D].rearrange("p (h t i) -> p h t i", h=H, t=2)
                        for m in range(2):
                            table = rope[:, slot, j, n, m, :].rearrange("p (t i) -> p t i", t=2).unsqueeze(1)
                            pool.tensor_tensor(products[:, m, n * D:n * D + D].rearrange("p (h t i) -> p h t i", h=H, t=2),
                                               src if m == 0 else src[:, :, ::-1, :],
                                               table.broadcast_to([P, H, 2, DH // 2]), ALU.mult).then_inc(rope_mul, 1)

                def add_bias(i, c, j):
                    g, half, slot = at("proj", i, c)
                    if j == 0:
                        pool.wait_ge(x_in[slot], half * 16 + 16)
                    pool.tensor_tensor(x_sb[:, slot, j, :], x_sb[:, slot, j, :], bias[:, :], ALU.add)\
                        .then_inc(x_biased, 1)

                def step(i, c):
                    for kind, *x in order:
                        if not at(kind, i, c):
                            continue
                        if kind == "rope":
                            rotate(i, c, *x)
                        elif kind == "split":
                            for j in range(GT):
                                add_bias(i, c, j)

                if not first:
                    pool.wait_ge(weights_in, 16 * N_LOADS)
                schedule(pool, step)

            @block.tensor
            def _(pe):
                pe.sem_inc(f_done, F_DONE_CREDIT)
                pe.sem_inc(t_done, T_DONE_CREDIT)
                if first:
                    pe.sem_inc(q_done, Q_DONE_CREDIT)
                pe.wait_ge(weights_in, 16 * N_LOADS)
                pe.wait_ge(weights_set, 5)

                def turn(i, c, n, kc):
                    g, _, _ = at("turn", i, c)
                    use = t_uses.index(("turn", n, kc))
                    if kc == 0:
                        pe.wait_ge(xn_done, g * (norms * GT) + GT * (n + 1))
                    pe.wait_ge(t_free, g * len(t_uses) + (use + 1))
                    for j in range(GT):
                        mm = pe.transpose(ps_t[:, use % 2, P * j:P * j + P], xn[:, j, P * kc:P * kc + P], ident[:, :])
                    mm.then_inc(t_done, 1)

                def proj(i, c, j):
                    g, _, _ = at("proj", i, c)
                    use = t_uses.index(("proj", j))
                    if j == 0:
                        pe.wait_ge(y_split, g + 1)
                    pe.wait_ge(t_free, g * len(t_uses) + (use + 1))
                    for kc in range(KC):
                        for y_part, w_part in SPLITS:
                            mm = pe.matmul(ps_t[:, use % 2, :], y_parts[:, y_part, kc, P * j:P * j + P],
                                           w_mm[:, w_part, kc, :], start=kc == 0 and (y_part, w_part) == SPLITS[0],
                                           stop=kc == KC - 1 and (y_part, w_part) == SPLITS[-1])
                    mm.then_inc(t_done, 1)

                def inputs(i, c):
                    g, _, _ = at("s", i, c)
                    use = f_uses.index(("s",))
                    pe.wait_ge(t_free, g * len(t_uses) + (T_BANKS + t_uses.index(("turn", 0, KC - 1)) + 1))
                    wait_f_bank(pe, g, use)
                    for kc in range(KC):
                        for w_part, x_part in SPLITS:
                            mm = pe.matmul(ps_f[:, use % 2, :], win[:, w_part, kc, :], xt[:, 0, x_part, kc, :],
                                           start=kc == 0 and (w_part, x_part) == SPLITS[0],
                                           stop=kc == KC - 1 and (w_part, x_part) == SPLITS[-1])
                    mm.then_inc(f_done, 1)

                def hidden(i, c, j):
                    g, _, _ = at("hidden", i, c)
                    use = f_uses.index(("hidden", j))
                    if j == 0:
                        wait_f_taken(pe, g, ("s",))
                    wait_f_bank(pe, g, use)
                    pe.matmul(ps_f[:, use % 2, :], sel[:, j, :], s_parts[:, :], start=True, stop=True)\
                      .then_inc(f_done, 1)

                def inner_out(i, c):
                    g, _, _ = at("inner", i, c)
                    use = f_uses.index(("inner",))
                    wait_f_taken(pe, g, ("hidden", NE - 1))
                    wait_f_bank(pe, g, use)
                    for j in range(NE):
                        lane = slice(DH * (j % 4), DH * (j % 4) + DH)
                        mm = pe.matmul(ps_f[lane, use % 2, :], w2[:, j, :], hid[:, j, :], start=j < 4, stop=j >= NE - 4)
                    mm.then_inc(f_done, 1)

                def ffn(i, c, j):
                    g, _, _ = at("ffn", i, c)
                    use = f_uses.index(("ffn", j))
                    if j == 0:
                        wait_f_taken(pe, g, ("inner",))
                    wait_f_bank(pe, g, use)
                    pe.matmul(ps_f[:, use % 2, :], inner[:, P * j:P * j + P], w_out[:, :], start=True, stop=True)\
                      .then_inc(f_done, 1)

                def project(i, c, j, n):
                    g, _, _ = at("qkv", i, c)
                    use = q_uses.index(("qkv", j, n))
                    if use == 0:
                        pe.wait_ge(t_free, g * len(t_uses) + (T_BANKS + len(t_uses)))
                    pe.wait_ge(q_free, g * len(q_uses) + (use + 1))
                    for kc in range(KC):
                        for x_part, w_part in SPLITS:
                            mm = pe.matmul(ps_q[:, use % 2, :], xt[:, 1, x_part, kc, P * j:P * j + P],
                                           w_mm[:, w_part, kc, D * n:D * n + D],
                                           start=kc == 0 and (x_part, w_part) == SPLITS[0],
                                           stop=kc == KC - 1 and (x_part, w_part) == SPLITS[-1])
                    mm.then_inc(q_done, 1)

                def turn_heads(i, c, h):
                    g, _, _ = at("turn_qk", i, c)
                    if h == 0:
                        pe.wait_ge(rope_done, g * GT + (1 + GT))
                    pe.wait_ge(r_free, g * (2 * KC) + (h + 1))
                    for j in range(GT):
                        mm = pe.transpose(ps_r[:, h % 2, P * j:P * j + P], turned_in[:, j, P * h:P * h + P],
                                          ident[:, :])
                    mm.then_inc(r_done, 1)

                do = {"turn": turn, "proj": proj, "s": inputs, "hidden": hidden, "inner": inner_out, "ffn": ffn,
                      "qkv": project, "turn_qk": turn_heads}

                def step(i, c):
                    for kind, *x in order:
                        if kind in do and at(kind, i, c):
                            do[kind](i, c, *x)

                schedule(pe, step)

            @block.scalar
            def _(act):
                act.sem_inc(f_free["act"], SLOT_CREDIT)
                if first:
                    act.sem_inc(qk_out[0], QK_OUT_CREDIT)
                    act.sem_inc(qk_out[1], QK_OUT_CREDIT)
                act.wait_ge(weights_in, 16 * N_LOADS)

                def norm(i, c, n):
                    g, _, _ = at("norm", i, c)
                    act.wait_ge(ticks, g * (norms * NORM_TICKS) + (NORM_TICKS * n + STAT_TICKS))
                    act.activation(std[:, :], var_eps[:, :], ACT.Sqrt).then_inc(std_done, 1)

                def turn(i, c, n, kc):
                    g, _, _ = at("turn", i, c)
                    use = t_uses.index(("turn", n, kc))
                    act.wait_ge(t_done, g * len(t_uses) + (T_DONE_CREDIT + use + 1))
                    if kc == 0:
                        if n == 0:
                            act.wait_ge(f_done, g * n_f + (F_DONE_CREDIT - n_f + f_uses.index(("s",)) + 1))
                        else:
                            act.wait_ge(q_done, g * len(q_uses) + Q_DONE_CREDIT)
                    act.copy(xt[:, n, 0, kc, :], ps_t[:, use % 2, :]).then_inc(t_first, 1)

                def split(i, c):
                    g, half, slot = at("split", i, c)
                    act.wait_ge(y_in[slot], half * 16 + 16)
                    act.wait_ge(t_done, g * len(t_uses) + (T_DONE_CREDIT + GT - len(t_uses)))
                    act.copy(y_parts[:, 0, :, :], y_sb[:, slot, :, :]).then_inc(y_first, 1)

                def inputs(i, c):
                    g, _, _ = at("s", i, c)
                    use = f_uses.index(("s",))
                    act.wait_ge(f_done, g * n_f + (F_DONE_CREDIT + use + 1))
                    act.activation(s_parts[:, :], ps_f[:, use % 2, :], ACT.Identity, bias=b_in[:, 0:1])\
                       .then_inc(s_first, 1)

                def hidden(i, c, j):
                    g, _, _ = at("hidden", i, c)
                    use = f_uses.index(("hidden", j))
                    act.wait_ge(f_done, g * n_f + (F_DONE_CREDIT + use + 1))
                    act.activation(hid[:, j, :], ps_f[:, use % 2, :], ACT.Relu, bias=b1[:, j:j + 1],
                                   scale=w1[:, j:j + 1]).then_inc(f_free["act"], 1)

                def inner_out(i, c):
                    g, _, _ = at("inner", i, c)
                    use = f_uses.index(("inner",))
                    act.wait_ge(f_done, g * n_f + (F_DONE_CREDIT + use + 1))
                    act.activation(inner[:, :], ps_f[:, use % 2, :], ACT.Identity, bias=b2[:, 0:1])\
                       .then_inc(f_free["act"], 1)

                def turn_heads(i, c, h):
                    g, _, _ = at("turn_qk", i, c)
                    act.wait_ge(r_done, g * (2 * KC) + (h + 1))
                    act.wait_ge(qk_out[h % 2], g * (32 * KC) + (32 * (h // 2) + QK_OUT_CREDIT))
                    act.copy(qk_parts[:, h % 2, 0, :], ps_r[:, h % 2, :]).then_inc(r_first, 1)

                do = {"norm": norm, "turn": turn, "split": split, "s": inputs, "hidden": hidden, "inner": inner_out,
                      "turn_qk": turn_heads}

                def step(i, c):
                    for kind, *x in order:
                        if kind in do and at(kind, i, c):
                            do[kind](i, c, *x)

                schedule(act, step)

            @block.vector
            def _(dve):
                dve.sem_inc(t_free, T_BANKS)
                dve.sem_inc(f_free["dve"], SLOT_CREDIT)
                if first:
                    dve.sem_inc(q_free, Q_BANKS)
                    dve.sem_inc(r_free, R_BANKS)
                    dve.sem_inc(rope_done, 1)
                    dve.sem_inc(v_out, V_OUT_CREDIT)
                dve.wait_ge(weights_in, 16 * N_LOADS)
                dve.tensor_copy(sel[:, :, :], sel32[:, :, :]).then_inc(weights_set, 1)
                dve.tensor_copy(win[:, 0, :, :], win32[:, :, :]).then_inc(weights_set, 1)
                dve.tensor_copy(w_mm[:, 0, :, :], stage[:, :, :]).then_inc(weights_set, 1)
                dve.wait_ge(weights_set, 3)
                dve.tensor_tensor(win[:, 1, :, :], win32[:, :, :], win[:, 0, :, :].bitcast(F32), ALU.subtract)\
                   .then_inc(weights_set, 1)
                dve.tensor_tensor(w_mm[:, 1, :, :], stage[:, :, :], w_mm[:, 0, :, :].bitcast(F32), ALU.subtract)\
                   .then_inc(weights_set, 1)
                dve.wait_ge(weights_set, 5)

                def statistics(i, c, n):
                    g, half, slot = at("stats", i, c)
                    base = NORM_TICKS * n

                    def tick(m):
                        dve.wait_ge(ticks, g * (norms * NORM_TICKS) + (base + m))
                    if not first:
                        dve.wait_ge(t_free, g * len(t_uses) + (T_BANKS + GT))
                    elif n == 0:
                        dve.wait_ge(x_in[slot], half * 16 + 16)
                    else:
                        wait_f_taken(dve, g, ("ffn", GT - 1))
                    def aggregate(j):
                        dve.bn_aggr(mean_var[:, j, :], stats[:, j, :]).then_inc(ticks, 1)

                    def add_eps(j):
                        dve.tensor_scalar(var_eps[:, j:j + 1], mean_var[:, j, 1:2], EPS, None, ALU.add)\
                           .then_inc(ticks, 1)

                    for j in range(GT):
                        if j >= 2:
                            tick(j - 1)
                        dve.bn_stats(stats[:, j, :], x_sb[:, slot, j, :]).then_inc(ticks, 1)
                        if j >= 2:
                            aggregate(j - 2)
                    tick(GT)
                    add_eps(0)
                    aggregate(2)
                    tick(GT + 2)
                    add_eps(1)
                    aggregate(3)
                    tick(GT + 4)
                    add_eps(2)
                    tick(GT + 6)
                    add_eps(3)

                def norm(i, c, n):
                    g, _, slot = at("norm", i, c)
                    base = NORM_TICKS * n + STAT_TICKS

                    def tick(m):
                        dve.wait_ge(ticks, g * (norms * NORM_TICKS) + (base + m))
                    dve.wait_ge(std_done, g * norms + (n + 1))
                    dve.reciprocal(rstd[:, 0, :], std[:, :]).then_inc(ticks, 1)
                    tick(1)
                    dve.tensor_tensor(rstd[:, 1, :], rstd[:, 0, :], rstd[:, 0, :], ALU.mult).then_inc(ticks, 1)
                    tick(2)
                    dve.tensor_tensor(rstd[:, 2, :], rstd[:, 1, :], var_eps[:, :], ALU.mult).then_inc(ticks, 1)
                    tick(3)
                    dve.tensor_scalar(rstd[:, 1, :], rstd[:, 2, :], -0.5, 1.5, ALU.mult, ALU.add).then_inc(ticks, 1)
                    tick(4)
                    dve.tensor_tensor(rstd[:, 3, :], rstd[:, 0, :], rstd[:, 1, :], ALU.mult).then_inc(ticks, 1)
                    tick(5)
                    for j in range(GT):
                        dve.tensor_scalar(xn[:, j, :], x_sb[:, slot, j, :], mean_var[:, j, 0:1], rstd[:, 3, j:j + 1],
                                          ALU.subtract, ALU.mult).then_inc(xn_done, 1)

                def turn(i, c, n, kc):
                    g, _, _ = at("turn", i, c)
                    use = t_uses.index(("turn", n, kc))
                    dve.wait_ge(t_first, g * (norms * KC) + (KC * n + kc + 1))
                    dve.tensor_tensor(xt[:, n, 1, kc, :], ps_t[:, use % 2, :], xt[:, n, 0, kc, :].bitcast(F32),
                                      ALU.subtract).then_inc(t_free, 1)

                def split(i, c):
                    g, _, slot = at("split", i, c)
                    dve.wait_ge(y_first, g + 1)
                    dve.tensor_tensor(y_parts[:, 1, :, :], y_sb[:, slot, :, :], y_parts[:, 0, :, :].bitcast(F32),
                                      ALU.subtract).then_inc(y_split, 1)

                def proj(i, c, j):
                    g, _, slot = at("proj", i, c)
                    use = t_uses.index(("proj", j))
                    dve.wait_ge(t_done, g * len(t_uses) + (T_DONE_CREDIT + use + 1))
                    dve.wait_ge(x_biased, g * GT + (j + 1))
                    dve.tensor_tensor(x_sb[:, slot, j, :], ps_t[:, use % 2, :], x_sb[:, slot, j, :], ALU.add)\
                       .then_inc(t_free, 1)

                def inputs(i, c):
                    g, _, _ = at("s", i, c)
                    use = f_uses.index(("s",))
                    dve.wait_ge(s_first, g + 1)
                    dve.scalar_tensor_tensor(out=s_parts[M:P, :], in0=ps_f[M:P, use % 2, :], scalar=b_in[M:P, 0:1],
                                             in1=s_parts[M:P, :].bitcast(F32), op0=ALU.add, op1=ALU.subtract)\
                       .then_inc(f_free["dve"], 1)

                def ffn(i, c, j):
                    g, _, slot = at("ffn", i, c)
                    use = f_uses.index(("ffn", j))
                    dve.wait_ge(f_done, g * n_f + (F_DONE_CREDIT + use + 1))
                    dve.scalar_tensor_tensor(out=x_sb[:, slot, j, :], in0=ps_f[:, use % 2, :], scalar=0.5,
                                             in1=x_sb[:, slot, j, :], op0=ALU.mult, op1=ALU.add)\
                       .then_inc(f_free["dve"], 1)

                def project(i, c, j, n):
                    g, _, _ = at("qkv", i, c)
                    use = q_uses.index(("qkv", j, n))
                    if use == 2:
                        dve.wait_ge(v_out, g * 16 + V_OUT_CREDIT)
                    dve.wait_ge(q_done, g * len(q_uses) + (Q_DONE_CREDIT + use + 1))
                    dve.tensor_tensor(qkv[:, j, D * n:D * n + D], ps_q[:, use % 2, :], bias[:, D * n:D * n + D], ALU.add)\
                       .then_inc(q_free, 1)

                def rotate(i, c, j):
                    g, _, _ = at("rope", i, c)
                    dve.wait_ge(rope_mul, g * (4 * GT) + 4 * (j + 1))
                    dve.tensor_tensor(turned_in[:, j, :], products[:, 0, :], products[:, 1, :], ALU.add)\
                       .then_inc(rope_done, 1)

                def turn_heads(i, c, h):
                    g, _, _ = at("turn_qk", i, c)
                    dve.wait_ge(r_first, g * (2 * KC) + (h + 1))
                    dve.tensor_tensor(qk_parts[:, h % 2, 1, :], ps_r[:, h % 2, :], qk_parts[:, h % 2, 0, :].bitcast(F32),
                                      ALU.subtract).then_inc(r_free, 1)

                do = {"stats": statistics, "norm": norm, "turn": turn, "split": split, "proj": proj, "s": inputs,
                      "ffn": ffn, "qkv": project, "rope": rotate, "turn_qk": turn_heads}

                def step(i, c):
                    for kind, *x in order:
                        if kind in do and at(kind, i, c):
                            do[kind](i, c, *x)

                schedule(dve, step)


N_IT = B * NHG
M_BANKS = 2
PAIRS = HG // 2
ST_PAIRS = 2
PT_SLOTS = 4
Q_ROWS = 3 * DH + 2


def main_steps():
    return [(g, j) for g in reversed(range(GB)) for j in range(GT * (g + 1))]


def max_steps():
    out, due = [], []
    for h in range(HG):
        for g in range(GB):
            for r in range(GT):
                for c in range(g + 1):
                    out.append(("chunk", h, g, r, c))
                    if due and len(out) >= due[0][0]:
                        out.append(due.pop(0)[1])
            due.append((len(out) + 4, ("rows", h, g)))
    return out + [d[1] for d in due]


def merged_steps(with_max=True):
    main, tops = main_steps(), max_steps() if with_max else []
    small = []
    for k in range(len(main) + 1):
        if k < len(main):
            small += [("st", k, 0), ("st", k, 1)]
        if k > 0:
            small += [("pv", k - 1), ("den", k - 1)]
    cost = {"st": 1.0, "pv": 2.0, "den": 2.0}

    def weight(step):
        g, j = main[step[1]]
        return cost[step[0]] * (GT - max(0, j - GT * g)) if step[1] >= 4 else 0.0
    whole = sum(weight(x) for x in small)
    out, done, n = [], 0.0, 0
    for x in small:
        out.append(x)
        done += weight(x)
        while n < min(len(tops), int(len(tops) * done / whole + 0.5)):
            out.append(tops[n])
            n += 1
    return out + tops[n:]


def attention(nc, qk_t, v_all, yt_all, ident_in, masks_in):
    main, tops = main_steps(), max_steps()
    n_main, n_tops, n_rows = len(main), len(tops), HG * GB
    both, main_only = merged_steps(), merged_steps(False)
    top_at = {s: i for i, s in enumerate(tops)}
    rows_order = [s for s in tops if s[0] == "rows"]
    unit_at = {s[1:]: i for i, s in enumerate(rows_order)}
    groups = list(reversed(range(GB)))

    with ExitStack() as ctx:
        def sb(name, shape, dt=F32):
            return ctx.enter_context(nc.sbuf_tensor(name, shape, dt))

        def psum(name, shape):
            return ctx.enter_context(nc.psum_tensor(name, shape, F32))

        def sem(name):
            return ctx.enter_context(nc.semaphore(name))

        ident = sb("a_ident", [P, P])
        masks32 = sb("a_masks32", [P, 2, P])
        ident_bf = sb("a_ident_bf", [P, P], BF16)
        masks_bf = sb("a_masks_bf", [P, 2, P], BF16)
        ones = sb("a_ones", [P, DH])
        q_sb = sb("q_sb", [Q_ROWS, 2, HG, S], F32R)
        k_sb = sb("k_sb", [Q_ROWS, 2, HG, S], F32R)
        v_sb = sb("v_sb", [P, 2, S // P, P])
        probs = sb("probs", [P, PT_SLOTS, HG, GTOK])
        y_raw = sb("y_raw", [P, 2, 2, GTOK])
        rdenom = sb("rdenom", [P, 2, GTOK])
        y_sb = sb("y_sb", [P, 2, GTOK])
        chunk_max = sb("chunk_max", [P, 2, GT, GB])
        neg_max = sb("neg_max", [P, 2, GT])
        neg_parts = sb("neg_parts", [P, 2, GT, 2])

        ps_max = psum("ps_max", [P, M_BANKS, GTOK])
        ps_st = psum("ps_st", [P, ST_PAIRS, 2, GTOK])
        ps_y = psum("ps_y", [P, GTOK])
        ps_den = psum("ps_den", [P, GTOK])

        consts_in = sem("a_consts_in")
        consts_set = sem("a_consts_set")
        pool_done = sem("a_pool_done")
        qk_in = [sem("qk_in0"), sem("qk_in1")]
        v_in = [sem("v_in0"), sem("v_in1")]
        y_out = [sem("y_out0"), sem("y_out1")]
        scored = sem("scored")
        max_free = sem("max_free")
        tops_done = sem("tops_done")
        rows_ready = sem("rows_ready")
        st_done = sem("st_done")
        exp_done = sem("exp_done")
        pv_done = sem("pv_done")
        y_taken = sem("y_taken")
        den_done = sem("den_done")
        y_done = sem("y_done")
        Y_CREDIT, Y_OUT_CREDIT, Y_DONE_CREDIT = 1, 1, 2

        with nc.Block() as block:

            @block.sync
            def _(sp):
                sp.dma_start(ident[:, :], ident_in).then_inc(consts_in, 16)
                sp.dma_start(masks32[:, :, :], masks_in).then_inc(consts_in, 16)

                def load(b, hg, a):
                    for tile, half, parts in ((q_sb, 0, (0, 0, 1)), (k_sb, NHG, (0, 1, 0))):
                        for n, part in enumerate(parts):
                            src = qk_t[hg + half, part, :, bass.ds(b * S, S)]
                            sp.dma_start(tile[DH * n:DH * n + DH, a, :, :].bitcast(F32),
                                         src.rearrange("(h d) s -> d h s", h=HG)).then_inc(qk_in[a], 16)
                    src = v_all[bass.ds(b * S, S), hg * P:hg * P + P]
                    sp.dma_start(v_sb[:, a, :, :], src.rearrange("(j p) c -> p j c", p=P)).then_inc(v_in[a], 16)

                def store(b, hg, n):
                    sp.wait_ge(y_done, b * (NHG * GB) + (hg * GB + Y_DONE_CREDIT + n + 1))
                    dst = yt_all[bass.ds(b * GB + groups[n], 1), hg, :, :]
                    sp.dma_start(dst.rearrange("o p s -> (o p) s"), y_sb[:, n % 2, :]).then_inc(y_out[n % 2], 16)

                def batch(b, last):
                    for hg in range(NHG):
                        for n in range(GB - 1):
                            store(b, hg, n)
                        if hg + 2 < NHG or not last:
                            sp.wait_ge(pv_done, b * (NHG * n_main) + (hg * n_main + PT_SLOTS + n_main))
                            load(b + (hg + 2) // NHG, (hg + 2) % NHG, hg % 2)
                        store(b, hg, GB - 1)

                load(0, 0, 0)
                load(0, 1, 1)
                with sp.Fori(0, B - 1) as b:
                    batch(b, False)
                batch(B - 1, True)
                for n in range(2):
                    sp.wait_ge(y_out[n], 16 * (Y_OUT_CREDIT + N_IT * GB // 2))

            @block.gpsimd
            def _(pool):
                for a in range(2):
                    pool.memset(k_sb[3 * DH:Q_ROWS, a, :, :].bitcast(F32), 1.0).then_inc(pool_done, 1)
                    pool.wait_ge(pool_done, a + 1)
                pool.memset(ones[:, :], 1.0).then_inc(pool_done, 1)
                pool.sem_inc(y_done, Y_DONE_CREDIT)
                pool.sem_inc(y_out[0], 16 * Y_OUT_CREDIT)
                pool.sem_inc(y_out[1], 16 * Y_OUT_CREDIT)
                with pool.Fori(0, N_IT) as it:
                    for n in range(GB):
                        pool.wait_ge(den_done, it * (GB * GT) + GT * (n + 1))
                        pool.wait_ge(y_out[n % 2], it * (16 * GB // 2) + 16 * (n // 2 + 1))
                        pool.tensor_tensor(y_sb[:, n % 2, :], y_raw[:, n % 2, 0, :], rdenom[:, n % 2, :],
                                           ALU.mult).then_inc(y_done, 1)

            @block.tensor
            def _(pe):
                pe.sem_inc(pv_done, PT_SLOTS)
                pe.wait_ge(consts_in, 32)
                pe.wait_ge(consts_set, 2)
                pe.wait_ge(pool_done, 3)

                def chunk(im, loads, a, step):
                    _, h, g, r, c = step
                    n = top_at[step]
                    if n == 0:
                        pe.wait_ge(qk_in[a], loads * (6 * 16))
                    pe.wait_ge(max_free, im * n_tops + (n + 1))
                    diagonal = c == g
                    width = (r + 1) * P if diagonal else GTOK
                    row = GTOK * g + P * r
                    mm = pe.matmul(ps_max[:, n % M_BANKS, 0:width], q_sb[0:3 * DH, a, h, row:row + P],
                                   k_sb[0:3 * DH, a, h, GTOK * c:GTOK * c + width], start=True, stop=not diagonal)
                    if diagonal:
                        mm = pe.matmul(ps_max[:, n % M_BANKS, P * r:P * r + P], ident_bf[:, :], masks_bf[:, 0, :],
                                       start=False, stop=True)
                    mm.then_inc(scored, 1)

                def rows(im, step):
                    n, u = top_at[step], unit_at[step[1:]]
                    pe.wait_ge(max_free, im * n_tops + (n + 1))
                    pe.wait_ge(rows_ready, im * n_rows + (u + 1))
                    for r in range(GT):
                        mm = pe.transpose(ps_max[0:2, n % M_BANKS, P * r:P * r + P], neg_parts[:, u % 2, r, :],
                                          ident[:, :])
                    mm.then_inc(scored, 1)

                def scores_t(it, a, k, p):
                    g, j = main[k]
                    n = PAIRS * k + p
                    if n == 0:
                        pe.wait_ge(max_free, it * n_tops + (M_BANKS + n_tops))
                    pe.wait_ge(exp_done, it * (PAIRS * n_main) + (n + 1))
                    c0 = P * max(0, j - GT * g)
                    for i in range(2):
                        h = 2 * p + i
                        out = ps_st[:, n % ST_PAIRS, i, :]
                        diagonal = j >= GT * g
                        mm = pe.matmul(out[:, c0:GTOK], k_sb[:, a, h, P * j:P * j + P],
                                       q_sb[:, a, h, GTOK * g + c0:GTOK * g + GTOK], start=True, stop=not diagonal)
                        if diagonal:
                            mm = pe.matmul(out[:, c0:c0 + P], ident_bf[:, :], masks_bf[:, 1, :], start=False,
                                           stop=True)
                    mm.then_inc(st_done, 1)

                def products(it, loads, a, k, den):
                    g, j = main[k]
                    if not den:
                        if k == 0:
                            pe.wait_ge(v_in[a], loads * 16)
                        if j == 0:
                            pe.wait_ge(y_taken, it * GB + (Y_CREDIT + groups.index(g)))
                        pe.wait_ge(exp_done, it * (PAIRS * n_main) + (ST_PAIRS + PAIRS * k + PAIRS))
                    c0 = P * max(0, j - GT * g)
                    last = j == GT * (g + 1) - 1
                    out = ps_den if den else ps_y
                    for h in range(HG):
                        rows = slice(DH * h, DH * h + DH)
                        mm = pe.matmul(out[rows, c0:GTOK], ones[:, :] if den else v_sb[:, a, j, rows],
                                       probs[:, k % PT_SLOTS, h, c0:GTOK], start=j == 0, stop=last)
                    if den:
                        mm.then_inc(pv_done, 1)

                def iteration(it, loads, a, ahead):
                    for step in both if ahead is not None else main_only:
                        if step[0] == "st":
                            scores_t(it, a, step[1], step[2])
                        elif step[0] in ("pv", "den"):
                            products(it, loads, a, step[1], step[0] == "den")
                        elif step[0] == "chunk":
                            chunk(it + 1, ahead, 1 - a, step)
                        else:
                            rows(it + 1, step)

                for step in tops:
                    if step[0] == "chunk":
                        chunk(0, 1, 0, step)
                    else:
                        rows(0, step)
                with pe.Fori(0, N_IT // 2 - 1) as i:
                    iteration(i * 2, i + 1, 0, i + 1)
                    iteration(i * 2 + 1, i + 1, 1, i + 2)
                iteration(N_IT - 2, N_IT // 2, 0, N_IT // 2)
                iteration(N_IT - 1, N_IT // 2, 1, None)

            @block.scalar
            def _(act):
                act.sem_inc(exp_done, ST_PAIRS)
                act.sem_inc(y_taken, Y_CREDIT)

                def exponentials(it, k):
                    g, j = main[k]
                    c0 = P * max(0, j - GT * g)
                    act.wait_ge(pv_done, it * n_main + (k + 1))
                    for p in range(PAIRS):
                        n = PAIRS * k + p
                        act.wait_ge(st_done, it * (PAIRS * n_main) + (n + 1))
                        act.activation(probs[:, k % PT_SLOTS, 2 * p:2 * p + 2, c0:GTOK],
                                       ps_st[:, n % ST_PAIRS, :, c0:GTOK], ACT.Exp).then_inc(exp_done, 1)

                def take_y(it, n):
                    done = sum(GT * (x + 1) for x in groups[:n + 1])
                    act.wait_ge(pv_done, it * n_main + (PT_SLOTS + done))
                    act.wait_ge(y_done, it * GB + (n + 1))
                    act.copy(y_raw[:, n % 2, 0, :], ps_y[:, :])
                    act.copy(y_raw[:, n % 2, 1, :], ps_den[:, :]).then_inc(y_taken, 1)

                with act.Fori(0, N_IT) as it:
                    for k, (g, j) in enumerate(main):
                        exponentials(it, k)
                        if j == 0 and k > 0:
                            take_y(it, groups.index(g) - 1)
                    take_y(it, GB - 1)

            @block.vector
            def _(dve):
                dve.sem_inc(max_free, M_BANKS)
                dve.wait_ge(consts_in, 32)
                dve.tensor_copy(ident_bf[:, :], ident[:, :]).then_inc(consts_set, 1)
                dve.tensor_copy(masks_bf[:, :, :], masks32[:, :, :]).then_inc(consts_set, 1)

                def take_max(im, step):
                    _, h, g, r, c = step
                    n, u = top_at[step], unit_at[h, g]
                    width = (r + 1) * P if c == g else GTOK
                    dve.wait_ge(scored, im * n_tops + (n + 1))
                    dve.tensor_reduce(chunk_max[:, u % 2, r, c:c + 1], ps_max[:, n % M_BANKS, 0:width], AX_X,
                                      ALU.max).then_inc(max_free, 1)
                    if r == GT - 1 and c == g:
                        base = im * (2 * n_rows) + 2 * u
                        dve.wait_ge(max_free, im * n_tops + (M_BANKS + n + 1))
                        dve.tensor_reduce(neg_max[:, u % 2, :], chunk_max[:, u % 2, :, 0:g + 1], AX_X, ALU.max,
                                          negate=True).then_inc(tops_done, 1)
                        high = neg_parts[:, u % 2, :, 0]
                        dve.wait_ge(tops_done, base + 1)
                        dve.tensor_copy(high.bitcast(F32R), neg_max[:, u % 2, :]).then_inc(tops_done, 1)
                        dve.wait_ge(tops_done, base + 2)
                        dve.tensor_tensor(neg_parts[:, u % 2, :, 1].bitcast(F32R), neg_max[:, u % 2, :], high,
                                          ALU.subtract).then_inc(rows_ready, 1)

                def take_rows(im, a, step):
                    _, h, g = step
                    n = top_at[step]
                    dve.wait_ge(scored, im * n_tops + (n + 1))
                    dve.tensor_copy(q_sb[3 * DH:Q_ROWS, a, h, GTOK * g:GTOK * g + GTOK],
                                    ps_max[0:2, n % M_BANKS, :]).then_inc(max_free, 1)

                def reciprocal(it, n, r):
                    if r == 0:
                        dve.wait_ge(y_taken, it * GB + (Y_CREDIT + n + 1))
                        dve.wait_ge(y_done, it * GB + (n + 1))
                    dve.reciprocal(rdenom[:, n % 2, P * r:P * r + P], y_raw[:, n % 2, 1, P * r:P * r + P])\
                       .then_inc(den_done, 1)

                def iteration(it, a, ahead):
                    due = []
                    for step in both if ahead else main_only:
                        if step[0] == "chunk":
                            take_max(it + 1, step)
                            if due:
                                reciprocal(it, *due.pop(0))
                        elif step[0] == "rows":
                            take_rows(it + 1, 1 - a, step)
                        elif step[0] == "den":
                            g, j = main[step[1]]
                            if j == GT * (g + 1) - 1:
                                due += [(groups.index(g), r) for r in range(GT)]
                    for x in due:
                        reciprocal(it, *x)

                for step in tops:
                    if step[0] == "chunk":
                        take_max(0, step)
                    else:
                        take_rows(0, 0, step)
                with dve.Fori(0, N_IT // 2 - 1) as i:
                    iteration(i * 2, 0, True)
                    iteration(i * 2 + 1, 1, True)
                iteration(N_IT - 2, 0, True)
                iteration(N_IT - 1, 1, False)


def macaron_block(nc, x, w, out):
    x_mid = nc.dram_tensor("x_mid", (TOK, D), F32).ap()
    qk_t = nc.dram_tensor("qk_t", (2 * NHG, 2, P, TOK), F32).ap()
    v_all = nc.dram_tensor("v_all", (TOK, D), F32).ap()
    yt_all = nc.dram_tensor("yt_all", (NG, NHG, P, GTOK), F32).ap()
    dense(nc, True, w, x, x_mid, None, qk_t, v_all)
    attention(nc, qk_t, v_all, yt_all, w["ident"], w["masks"])
    dense(nc, False, w, x_mid, out, yt_all, None, None)


def constants():
    c = {"ident": np.eye(P, dtype=np.float32)}
    lower = np.tril(np.ones((P, P), bool))
    c["masks"] = np.stack([np.where(lower, 0.0, MASK), np.where(lower.T, 0.0, MASK)], 1).astype(np.float32)
    unit = np.arange(NE * P) // INNER
    c["sel"] = (np.arange(P)[:, None] % M == unit[None, :]).astype(np.float32).reshape(P, NE, P)
    angles = np.arange(S, dtype=np.float32)[:, None] / np.float32(10000.0) ** (
        np.arange(0, DH, 2, dtype=np.float32) / np.float32(DH))
    cos, sin = np.cos(angles), np.sin(angles)
    own = np.concatenate([cos, sin], 1)
    other = np.concatenate([-(1 - cos), 1 - sin], 1)
    both = np.stack([own, other], 1)
    table = np.stack([both * np.float32(DH ** -0.5), both], 1).astype(np.float32)
    c["rope"] = np.tile(table.reshape(S, 4 * DH), (B, 1))
    return c


def kernel(L0_attn_x, L0_attn_Wqkv, L0_attn_bqkv, L0_attn_Wproj, L0_attn_bproj, L0_ffn_Win, L0_ffn_bin_, L0_ffn_W1,
           L0_ffn_b1, L0_ffn_W2, L0_ffn_b2, L0_ffn_Wout, L0_ffn_bout):
    import concourse.bacc as bacc
    from concourse.bass_utils import run_bass_kernel_spmd

    def heads(a):
        a = np.asarray(a).reshape((H, 3, DH) + np.asarray(a).shape[1:])
        qk = a[:, :2].reshape((H, 2, DH // 2, 2) + a.shape[3:])
        qk = np.moveaxis(qk, 3, 2).reshape((H, 2, DH) + a.shape[3:])
        return np.concatenate([qk, a[:, 2:]], 1).swapaxes(0, 1).reshape((3 * D,) + a.shape[3:])

    place = [DH * (m // 8 % 4) + 8 * (m // 32) + m % 8 for m in range(M)]
    w2 = np.zeros((P, NE, DH), np.float32)
    b2 = np.zeros((P, 1), np.float32)
    w_out = np.zeros((P, D), np.float32)
    for m in range(M):
        row = INNER * (m % 8)
        w2[row:row + INNER, m // 8, place[m] % DH] = np.asarray(L0_ffn_W2)[m]
        b2[place[m], 0] = np.asarray(L0_ffn_b2)[m]
        w_out[place[m]] = np.asarray(L0_ffn_Wout)[m]
    b2[DH // 2, 0] = 1.0
    w_out[DH // 2] = np.asarray(L0_ffn_bout)
    arrays = {
        "x": np.asarray(L0_attn_x).reshape(TOK, D),
        "w_qkv": heads(L0_attn_Wqkv).T, "b_qkv": heads(L0_attn_bqkv),
        "w_proj": np.asarray(L0_attn_Wproj).T, "b_proj": np.asarray(L0_attn_bproj),
        "w_in": np.asarray(L0_ffn_Win),
        "b_in": np.concatenate([np.asarray(L0_ffn_bin_)] * 2).reshape(P, 1),
        "w1": np.asarray(L0_ffn_W1).reshape(NE, P).T, "b1": np.asarray(L0_ffn_b1).reshape(NE, P).T,
        "w2": w2, "b2": b2, "w_out": w_out, **constants(),
    }
    arrays = {k: np.ascontiguousarray(v) for k, v in arrays.items()}

    nc = bacc.Bacc("TRN2", target_bir_lowering=False, num_devices=1)
    aps = {k: nc.dram_tensor("in_" + k, v.shape, F32, kind="ExternalInput").ap() for k, v in arrays.items()}
    out = nc.dram_tensor("out", (TOK, D), F32, kind="ExternalOutput").ap()
    macaron_block(nc, aps["x"], aps, out)
    result = run_bass_kernel_spmd(nc, [{"in_" + k: v for k, v in arrays.items()}], core_ids=[0])
    return result.results[0]["out"].reshape(B, S, D)
```

```python
from contextlib import ExitStack

import numpy as np

import concourse.bass as bass
from concourse import mybir

F32 = mybir.dt.float32
F32R = mybir.dt.float32r
BF16 = mybir.dt.bfloat16
ALU = mybir.AluOpType
ACT = mybir.ActivationFunctionType
AX_X = mybir.AxisListType.X

P = 128
B, S, D, H = 4, 2048, 512, 16
DH = D // H
TOK = B * S
M, INNER = 64, 16
KC = D // P
GT = 4
GTOK = GT * P
NG = TOK // GTOK
GB = S // GTOK
HG = 4
NHG = H // HG
NE = M * INNER // P
EPS = 1e-5
MASK = -3.0e38


SPLITS = ((0, 0), (0, 1), (1, 0))
T_BANKS = F_BANKS = Q_BANKS = R_BANKS = 2
STAT_TICKS = 3 * GT
NORM_TICKS = STAT_TICKS + 5
HALVES = 2 * GT
LATE = HALVES - 2
TURNED_SLOTS, PARTS_SLOTS = 2, 4


def order_first():
    q = [("qkv", j, n) for j in range(GT) for n in range(3)]
    rope = [("rope", j) for j in range(GT)]
    r = [("turn_qk" if h < LATE else "turn_late", h) for h in range(HALVES)]
    t = [[("turn", n, kc) for kc in range(KC)] for n in range(2)]
    e = [("hidden", j) for j in range(NE)]
    o = [("ffn", j) for j in range(GT)]
    return (q[0:1] + [("stats", 0)] + q[1:2] + [("norm", 0)] + r[6:8] + q[2:3] + t[0][0:2] + q[3:4] + t[0][2:4]
            + rope[0:1] + q[4:5] + [("s",)] + r[0:1] + q[5:6] + e[0:2] + r[1:2] + q[6:7] + e[2:4] + q[7:8] + rope[1:2]
            + e[4:6] + q[8:9] + e[6:8] + r[2:3] + [("inner",)] + r[3:4] + o + [("stats", 1)] + q[9:11]
            + [("norm", 1)] + q[11:12] + rope[2:3] + t[1][0:2] + r[4:6] + t[1][2:4] + rope[3:4])


def order_last():
    p = [("proj", j) for j in range(GT)]
    t = [("turn", 0, kc) for kc in range(KC)]
    e = [("hidden", j) for j in range(NE)]
    o = [("ffn", j) for j in range(GT)]
    return (p[0:1] + [("s",)] + p[1:2] + e[0:2] + p[2:3] + e[2:4] + p[3:4] + [("stats", 0)] + e[4:8] + [("split",)]
            + [("norm", 0), ("inner",)] + o + t)


def dense(nc, first, w, x_in_all, x_out_all, yt_all, qk_t, v_all):
    order = order_first() if first else order_last()
    name = "f_" if first else "l_"
    ffn_kinds = ("s", "hidden", "inner", "ffn")
    if first:
        offset = {k: 1 for k in ("stats", "norm", "turn") + ffn_kinds}
        offset.update(qkv=0, rope=0, reload=0, turn_qk=0, turn_late=-1)
    else:
        offset = {k: 1 for k in ("proj", "stats", "norm", "turn")}
        offset.update({k: 0 for k in ffn_kinds}, split=2)
    norms = sum(x[0] == "stats" for x in order)
    t_uses = [x for x in order if x[0] in ("proj", "turn")]
    f_uses = [x for x in order if x[0] in ffn_kinds]
    q_uses = [x for x in order if x[0] == "qkv"]
    f_owner = ["dve" if x[0] in ("s", "ffn") else "act" for x in f_uses]

    with ExitStack() as ctx:
        def sb(n, shape, dt=F32):
            return ctx.enter_context(nc.sbuf_tensor(name + n, shape, dt))

        def psum(n):
            return ctx.enter_context(nc.psum_tensor(name + n, [P, 2, GTOK], F32))

        def sem(n):
            return ctx.enter_context(nc.semaphore(name + n))

        ident = sb("ident", [P, P])
        sel = sb("sel", [P, NE, P], F32R)
        win = sb("win", [P, 2, KC, P], F32R)
        b_in = sb("b_in", [P, 1])
        w1 = sb("w1", [P, NE])
        b1 = sb("b1", [P, NE])
        w2 = sb("w2", [P, NE, DH])
        b2 = sb("b2", [P, 1])
        w_out = sb("w_out", [P, D])
        x_sb = sb("x_sb", [P, 2, GT, D])
        xn = sb("xn", [P, GT, D])
        stats = sb("stats", [P, GT, 6])
        mean_var = sb("mean_var", [P, GT, 2])
        var_eps = sb("var_eps", [P, GT])
        std = sb("std", [P, GT])
        rstd = sb("rstd", [P, 4, GT])
        n_xt = 2 if first else 1
        xt = sb("xt", [P, n_xt, 2, KC, GTOK], F32R)
        s_parts = sb("s_parts", [P, GTOK], F32R)
        hid = sb("hid", [P, NE, GTOK])
        inner = sb("inner", [P, GTOK])
        cols = 3 * D if first else D
        w_mm = sb("w_mm", [P, 2, KC, cols], F32R)
        bias = sb("bias", [P, cols])
        if first:
            qkv = sb("qkv", [P, GT, 3 * D])
            stage = qkv
            turned_in = sb("turned_in", [P, TURNED_SLOTS, 2 * D])
            products = sb("products", [P, 2, 2 * D])
            staged = products
            rope = sb("rope", [P, 2, GT, 2, 2, DH])
            qk_parts = sb("qk_parts", [P, PARTS_SLOTS, 2, GTOK], F32R)
        else:
            stage = sb("stage", [P, KC, D])
            staged = sb("staged", [P, 2, 2 * D])
            y_sb = sb("y_sb", [P, 2, KC, GTOK])
            x_raw = sb("x_raw", [P, 2, GT, D])
            y_parts = sb("y_parts", [P, 2, KC, GTOK], F32R)

        sel32 = staged[:, 0, :].rearrange("p (e q) -> p e q", e=NE)
        win32 = staged[:, 1, 0:KC * P].rearrange("p (k m) -> p k m", k=KC)

        ps_t, ps_f = psum("ps_t"), psum("ps_f")
        if first:
            ps_q, ps_r = psum("ps_q"), psum("ps_r")

        weights_in = sem("weights_in")
        w_mm_in = sem("w_mm_in")
        weights_set = sem("weights_set")
        x_in = [sem("x_in0"), sem("x_in1")]
        x_out = [sem("x_out0"), sem("x_out1")]
        ticks = sem("ticks")
        std_done = sem("std_done")
        xn_done = sem("xn_done")
        t_done = sem("t_done")
        t_first = sem("t_first")
        t_free = sem("t_free")
        f_done = sem("f_done")
        s_first = sem("s_first")
        f_free = {"dve": sem("f_free_dve"), "act": sem("f_free_act")}
        if first:
            rope_in = [sem("rope_in0"), sem("rope_in1")]
            v_out = sem("v_out")
            q_done = sem("q_done")
            q_free = sem("q_free")
            rope_mul = sem("rope_mul")
            rope_done = sem("rope_done")
            r_done = sem("r_done")
            r_first = sem("r_first")
            r_free = sem("r_free")
            qk_out = [sem("qk_out%d" % n) for n in range(PARTS_SLOTS)]
        else:
            y_in = [sem("y_in0"), sem("y_in1")]
            y_first = sem("y_first")
            y_split = sem("y_split")
            x_biased = sem("x_biased")

        n_f = len(f_uses)
        f_per = {e: f_owner.count(e) for e in f_free}
        f_nth = [f_owner[:i + 1].count(f_owner[i]) for i in range(n_f)]
        SLOT_CREDIT, F_DONE_CREDIT, Q_DONE_CREDIT, T_DONE_CREDIT = 2, 16, 1, 8
        V_OUT_CREDIT, QK_OUT_CREDIT, N_LOADS = 16, 32, 11
        X_OUT_CREDIT, R_DONE_CREDIT = 0 if first else 16, 2 * TURNED_SLOTS
        parts_uses = HALVES // PARTS_SLOTS

        def wait_f_bank(eng, g, n):
            m = n - F_BANKS
            owner = f_owner[m]
            nth = f_nth[m] - (f_per[owner] if m < 0 else 0)
            eng.wait_ge(f_free[owner], g * f_per[owner] + (SLOT_CREDIT + nth))

        def wait_f_taken(eng, g, use):
            n = f_uses.index(use)
            eng.wait_ge(f_free[f_owner[n]], g * f_per[f_owner[n]] + (SLOT_CREDIT + f_nth[n]))

        low, high = -max(offset.values()), NG - min(offset.values())
        mid_low, mid_high = -min(offset.values()), NG - 2 - (offset["reload"] if first else offset["split"])
        pairs = (mid_high - mid_low) // 2

        def schedule(eng, step):
            for c in range(low, mid_low):
                step(0, c)
            with eng.Fori(0, pairs) as i:
                step(i, mid_low)
                step(i, mid_low + 1)
            for c in range(mid_low + 2 * pairs, high):
                step(0, c)

        def at(kind, i, c):
            c += offset[kind]
            if isinstance(i, int) and not 0 <= c < NG:
                return None
            return i * 2 + c, i + c // 2, c % 2

        with nc.Block() as block:

            @block.sync
            def _(sp):
                def tokens(g):
                    return bass.ds(g * GTOK, GTOK)

                def load_x(g, slot):
                    dst = x_sb if first else x_raw
                    sp.dma_start(dst[:, slot, :, :], x_in_all[tokens(g), :].rearrange("(j p) d -> p j d", p=P))\
                      .then_inc(x_in[slot], 16)

                def load_y(g, slot):
                    sp.dma_start(y_sb[:, slot, :, :], yt_all[bass.ds(g, 1), :, :, :].rearrange(
                        "o h p s -> p (o h) s")).then_inc(y_in[slot], 16)

                def load_rope(g, slot):
                    sp.dma_start(rope[:, slot, :, :, :, :].rearrange("p j a b d -> p j (a b d)"),
                                 w["rope"][tokens(g), :].rearrange("(j p) c -> p j c", p=P)).then_inc(rope_in[slot], 16)

                if first:
                    load_x(0, 0)
                else:
                    load_y(0, 0)
                loads = [(ident[:, :], w["ident"]), (sel32[:, :, :], w["sel"]),
                         (win32[:, :, 0:M], w["w_in"].rearrange("(k p) m -> p k m", p=P)),
                         (win32[:, :, M:P], w["w_in"].rearrange("(k p) m -> p k m", p=P)),
                         (b_in[:, :], w["b_in"]), (w1[:, :], w["w1"]), (b1[:, :], w["b1"]),
                         (w2[:, :, :], w["w2"]), (b2[:, :], w["b2"]), (w_out[:, :], w["w_out"]),
                         (bias[:, :], (w["b_qkv"] if first else w["b_proj"]).partition_broadcast(P))]
                for dst, src in loads:
                    sp.dma_start(dst, src).then_inc(weights_in, 16)
                assert len(loads) == N_LOADS
                sp.dma_start(stage[:, :, :], (w["w_qkv"] if first else w["w_proj"]).rearrange("(k p) n -> p k n", p=P))\
                  .then_inc(w_mm_in, 16)
                if first:
                    load_rope(0, 0)
                    load_x(1, 1)
                    load_rope(1, 1)
                else:
                    load_x(0, 0)
                    load_y(1, 1)
                    load_x(1, 1)

                def store_qk(i, c, kind, some):
                    g, _, _ = at(kind, i, c)
                    for h in some:
                        tile, half = h // 2, h % 2
                        at_tokens = bass.ds(i * (2 * GTOK) + (GTOK * (c + offset[kind]) + P * tile), P)
                        sp.wait_ge(r_free, g * HALVES + (R_BANKS + h + 1))
                        for part in range(2):
                            dst = qk_t[NHG * half:NHG * half + NHG, part, :, at_tokens]
                            sp.dma_start(dst.rearrange("h p s -> p h s"),
                                         qk_parts[:, h % PARTS_SLOTS, part, :].bitcast(F32).rearrange(
                                             "p (h s) -> p h s", h=NHG)).then_inc(qk_out[h % PARTS_SLOTS], 16)

                def store_v(i, c):
                    g, _, slot = at("turn_late", i, c)
                    sp.wait_ge(q_free, g * (3 * GT) + (Q_BANKS + 3 * GT))
                    sp.dma_start(v_all[tokens(g), :].rearrange("(j p) d -> p j d", p=P),
                                 qkv[:, :, 2 * D:3 * D]).then_inc(v_out, 16)
                    if not isinstance(i, int) or g + 2 < NG:
                        sp.wait_ge(rope_mul, g * (4 * GT) + 4 * GT)
                        load_rope(g + 2, slot)

                def reload_x(i, c):
                    g, half, slot = at("reload", i, c)
                    if not isinstance(i, int) or g + 2 < NG:
                        sp.wait_ge(x_out[slot], half * 16 + 16)
                        sp.wait_ge(xn_done, g * (norms * GT) + norms * GT)
                        load_x(g + 2, slot)

                def store_x(i, c):
                    g, _, slot = at("ffn", i, c)
                    wait_f_taken(sp, g, ("ffn", GT - 1))
                    sp.dma_start(x_out_all[tokens(g), :].rearrange("(j p) d -> p j d", p=P), x_sb[:, slot, :, :])\
                      .then_inc(x_out[slot], 16)

                def reload_x_raw(i, c):
                    g, _, slot = at("proj", i, c)
                    if not isinstance(i, int) or g + 2 < NG:
                        sp.wait_ge(x_biased, g * GT + GT)
                        load_x(g + 2, slot)

                def reload_y(i, c):
                    g, _, slot = at("split", i, c)
                    if not isinstance(i, int) or g + 2 < NG:
                        sp.wait_ge(y_split, g + 1)
                        load_y(g + 2, slot)

                def step(i, c):
                    if first:
                        if at("reload", i, c):
                            reload_x(i, c)
                        if at("turn_late", i, c):
                            store_v(i, c)
                            store_qk(i, c, "turn_late", range(LATE, HALVES))
                        if at("turn_qk", i, c):
                            store_qk(i, c, "turn_qk", range(LATE - 2))
                        if at("ffn", i, c):
                            store_x(i, c)
                        if at("turn_qk", i, c):
                            store_qk(i, c, "turn_qk", range(LATE - 2, LATE))
                    else:
                        if at("proj", i, c):
                            reload_x_raw(i, c)
                        if at("split", i, c):
                            reload_y(i, c)
                        if at("ffn", i, c):
                            store_x(i, c)

                schedule(sp, step)
                for slot in range(2):
                    sp.wait_ge(x_out[slot], X_OUT_CREDIT + 16 * (NG // 2))
                if first:
                    for slot in range(PARTS_SLOTS):
                        sp.wait_ge(qk_out[slot], QK_OUT_CREDIT + NG * parts_uses * 32)
                    sp.wait_ge(v_out, V_OUT_CREDIT + 16 * NG)

            @block.gpsimd
            def _(pool):
                def rotate(i, c, j):
                    g, half, slot = at("rope", i, c)
                    if j == 0:
                        pool.wait_ge(rope_in[slot], half * 16 + 16)
                    pool.wait_ge(q_free, g * (3 * GT) + (Q_BANKS + 3 * j + 2))
                    pool.wait_ge(rope_done, g * GT + (1 + j))
                    for n in range(2):
                        src = qkv[:, j, n * D:n * D + D].rearrange("p (h t i) -> p h t i", h=H, t=2)
                        for m in range(2):
                            table = rope[:, slot, j, n, m, :].rearrange("p (t i) -> p t i", t=2).unsqueeze(1)
                            dst = products[:, m, n * D:n * D + D].rearrange("p (h t i) -> p h t i", h=H, t=2)
                            pool.tensor_tensor(dst, src if m == 0 else src[:, :, ::-1, :],
                                               table.broadcast_to([P, H, 2, DH // 2]), ALU.mult).then_inc(rope_mul, 1)

                def add_bias(i, c):
                    g, half, slot = at("proj", i, c)
                    pool.wait_ge(x_in[slot], half * 16 + 16)
                    pool.wait_ge(x_out[slot], half * 16 + X_OUT_CREDIT)
                    for j in range(GT):
                        pool.tensor_tensor(x_sb[:, slot, j, :], x_raw[:, slot, j, :], bias[:, :], ALU.add)\
                            .then_inc(x_biased, 1)

                def split(i, c):
                    g, _, slot = at("split", i, c)
                    pool.wait_ge(y_first, g + 1)
                    pool.tensor_tensor(y_parts[:, 1, :, :], y_sb[:, slot, :, :], y_parts[:, 0, :, :].bitcast(F32),
                                       ALU.subtract).then_inc(y_split, 1)

                def step(i, c):
                    for kind, *x in order:
                        if not at(kind, i, c):
                            continue
                        if kind == "rope":
                            rotate(i, c, *x)
                        elif kind == "split":
                            split(i, c)
                        elif kind == "proj" and x[0] == 0:
                            add_bias(i, c)

                if not first:
                    pool.sem_inc(x_out[0], X_OUT_CREDIT)
                    pool.sem_inc(x_out[1], X_OUT_CREDIT)
                    pool.wait_ge(weights_in, 16 * N_LOADS)
                schedule(pool, step)

            @block.tensor
            def _(pe):
                pe.sem_inc(f_done, F_DONE_CREDIT)
                pe.sem_inc(t_done, T_DONE_CREDIT)
                if first:
                    pe.sem_inc(q_done, Q_DONE_CREDIT)
                    pe.sem_inc(r_done, R_DONE_CREDIT)
                pe.wait_ge(weights_in, 16 * N_LOADS)
                pe.wait_ge(weights_set, 3)

                def turn(i, c, n, kc):
                    g, _, _ = at("turn", i, c)
                    use = t_uses.index(("turn", n, kc))
                    if kc == 0:
                        pe.wait_ge(xn_done, g * (norms * GT) + GT * (n + 1))
                    pe.wait_ge(t_free, g * len(t_uses) + (use + 1))
                    for j in range(GT):
                        mm = pe.transpose(ps_t[:, use % 2, P * j:P * j + P], xn[:, j, P * kc:P * kc + P], ident[:, :])
                    mm.then_inc(t_done, 1)

                def proj(i, c, j):
                    g, _, _ = at("proj", i, c)
                    use = t_uses.index(("proj", j))
                    if j == 0:
                        pe.wait_ge(y_split, g + 1)
                    pe.wait_ge(t_free, g * len(t_uses) + (use + 1))
                    for kc in range(KC):
                        for y_part, w_part in SPLITS:
                            mm = pe.matmul(ps_t[:, use % 2, :], y_parts[:, y_part, kc, P * j:P * j + P],
                                           w_mm[:, w_part, kc, :], start=kc == 0 and (y_part, w_part) == SPLITS[0],
                                           stop=kc == KC - 1 and (y_part, w_part) == SPLITS[-1])
                    mm.then_inc(t_done, 1)

                def inputs(i, c):
                    g, _, _ = at("s", i, c)
                    use = f_uses.index(("s",))
                    pe.wait_ge(t_free, g * len(t_uses) + (T_BANKS + t_uses.index(("turn", 0, KC - 1)) + 1))
                    wait_f_bank(pe, g, use)
                    for kc in range(KC):
                        for w_part, x_part in SPLITS:
                            mm = pe.matmul(ps_f[:, use % 2, :], win[:, w_part, kc, :], xt[:, 0, x_part, kc, :],
                                           start=kc == 0 and (w_part, x_part) == SPLITS[0],
                                           stop=kc == KC - 1 and (w_part, x_part) == SPLITS[-1])
                    mm.then_inc(f_done, 1)

                def hidden(i, c, j):
                    g, _, _ = at("hidden", i, c)
                    use = f_uses.index(("hidden", j))
                    if j == 0:
                        wait_f_taken(pe, g, ("s",))
                    wait_f_bank(pe, g, use)
                    pe.matmul(ps_f[:, use % 2, :], sel[:, j, :], s_parts[:, :], start=True, stop=True)\
                      .then_inc(f_done, 1)

                def inner_out(i, c):
                    g, _, _ = at("inner", i, c)
                    use = f_uses.index(("inner",))
                    wait_f_taken(pe, g, ("hidden", NE - 1))
                    wait_f_bank(pe, g, use)
                    for j in range(NE):
                        lane = slice(DH * (j % 4), DH * (j % 4) + DH)
                        mm = pe.matmul(ps_f[lane, use % 2, :], w2[:, j, :], hid[:, j, :], start=j < 4, stop=j >= NE - 4)
                    mm.then_inc(f_done, 1)

                def ffn(i, c, j):
                    g, _, _ = at("ffn", i, c)
                    use = f_uses.index(("ffn", j))
                    if j == 0:
                        wait_f_taken(pe, g, ("inner",))
                    wait_f_bank(pe, g, use)
                    pe.matmul(ps_f[:, use % 2, :], inner[:, P * j:P * j + P], w_out[:, :], start=True, stop=True)\
                      .then_inc(f_done, 1)

                def project(i, c, j, n):
                    g, _, _ = at("qkv", i, c)
                    use = q_uses.index(("qkv", j, n))
                    if use == 0:
                        pe.wait_ge(t_free, g * len(t_uses) + (T_BANKS + len(t_uses)))
                    pe.wait_ge(q_free, g * len(q_uses) + (use + 1))
                    for kc in range(KC):
                        for x_part, w_part in SPLITS:
                            mm = pe.matmul(ps_q[:, use % 2, :], xt[:, 1, x_part, kc, P * j:P * j + P],
                                           w_mm[:, w_part, kc, D * n:D * n + D],
                                           start=kc == 0 and (x_part, w_part) == SPLITS[0],
                                           stop=kc == KC - 1 and (x_part, w_part) == SPLITS[-1])
                    mm.then_inc(q_done, 1)

                def turn_heads(i, c, h):
                    g, _, _ = at("turn_qk" if h < LATE else "turn_late", i, c)
                    tile, half = h // 2, h % 2
                    if half == 0:
                        pe.wait_ge(rope_done, g * GT + (1 + tile + 1))
                    pe.wait_ge(r_free, g * HALVES + (h + 1))
                    for hg in range(NHG):
                        mm = pe.transpose(ps_r[:, h % 2, P * hg:P * hg + P],
                                          turned_in[:, tile % TURNED_SLOTS, D * half + P * hg:D * half + P * hg + P],
                                          ident[:, :])
                    mm.then_inc(r_done, 1)

                do = {"turn": turn, "proj": proj, "s": inputs, "hidden": hidden, "inner": inner_out, "ffn": ffn,
                      "qkv": project, "turn_qk": turn_heads, "turn_late": turn_heads}

                def step(i, c):
                    if c == low + 1:
                        pe.wait_ge(weights_set, 5)
                    for kind, *x in order:
                        if kind in do and at(kind, i, c):
                            do[kind](i, c, *x)

                schedule(pe, step)

            @block.scalar
            def _(act):
                act.sem_inc(f_free["act"], SLOT_CREDIT)
                if first:
                    for slot in range(PARTS_SLOTS):
                        act.sem_inc(qk_out[slot], QK_OUT_CREDIT)
                act.wait_ge(weights_in, 16 * N_LOADS)

                def norm(i, c, n):
                    g, _, _ = at("norm", i, c)
                    act.wait_ge(ticks, g * (norms * NORM_TICKS) + (NORM_TICKS * n + STAT_TICKS))
                    act.activation(std[:, :], var_eps[:, :], ACT.Sqrt).then_inc(std_done, 1)

                def turn(i, c, n, kc):
                    g, _, _ = at("turn", i, c)
                    use = t_uses.index(("turn", n, kc))
                    act.wait_ge(t_done, g * len(t_uses) + (T_DONE_CREDIT + use + 1))
                    if kc == 0:
                        if n == 0:
                            act.wait_ge(f_done, g * n_f + (F_DONE_CREDIT - n_f + f_uses.index(("s",)) + 1))
                        else:
                            act.wait_ge(q_done, g * len(q_uses) + Q_DONE_CREDIT)
                    act.copy(xt[:, n, 0, kc, :], ps_t[:, use % 2, :]).then_inc(t_first, 1)

                def split(i, c):
                    g, half, slot = at("split", i, c)
                    act.wait_ge(y_in[slot], half * 16 + 16)
                    act.wait_ge(t_done, g * len(t_uses) + (T_DONE_CREDIT + GT - len(t_uses)))
                    act.copy(y_parts[:, 0, :, :], y_sb[:, slot, :, :]).then_inc(y_first, 1)

                def inputs(i, c):
                    g, _, _ = at("s", i, c)
                    use = f_uses.index(("s",))
                    act.wait_ge(f_done, g * n_f + (F_DONE_CREDIT + use + 1))
                    act.activation(s_parts[:, :], ps_f[:, use % 2, :], ACT.Identity, bias=b_in[:, 0:1])\
                       .then_inc(s_first, 1)

                def hidden(i, c, j):
                    g, _, _ = at("hidden", i, c)
                    use = f_uses.index(("hidden", j))
                    act.wait_ge(f_done, g * n_f + (F_DONE_CREDIT + use + 1))
                    act.activation(hid[:, j, :], ps_f[:, use % 2, :], ACT.Relu, bias=b1[:, j:j + 1],
                                   scale=w1[:, j:j + 1]).then_inc(f_free["act"], 1)

                def inner_out(i, c):
                    g, _, _ = at("inner", i, c)
                    use = f_uses.index(("inner",))
                    act.wait_ge(f_done, g * n_f + (F_DONE_CREDIT + use + 1))
                    act.activation(inner[:, :], ps_f[:, use % 2, :], ACT.Identity, bias=b2[:, 0:1])\
                       .then_inc(f_free["act"], 1)

                def turn_heads(i, c, h):
                    g, _, _ = at("turn_qk" if h < LATE else "turn_late", i, c)
                    act.wait_ge(r_done, g * HALVES + (R_DONE_CREDIT + h + 1))
                    slot = h % PARTS_SLOTS
                    act.wait_ge(qk_out[slot], g * (32 * parts_uses) + (32 * (h // PARTS_SLOTS) + QK_OUT_CREDIT))
                    act.copy(qk_parts[:, slot, 0, :], ps_r[:, h % 2, :]).then_inc(r_first, 1)

                do = {"norm": norm, "turn": turn, "split": split, "s": inputs, "hidden": hidden, "inner": inner_out,
                      "turn_qk": turn_heads, "turn_late": turn_heads}

                def step(i, c):
                    for kind, *x in order:
                        if kind in do and at(kind, i, c):
                            do[kind](i, c, *x)

                schedule(act, step)

            @block.vector
            def _(dve):
                dve.sem_inc(t_free, T_BANKS)
                dve.sem_inc(f_free["dve"], SLOT_CREDIT)
                if first:
                    dve.sem_inc(q_free, Q_BANKS)
                    dve.sem_inc(r_free, R_BANKS)
                    dve.sem_inc(rope_done, 1)
                    dve.sem_inc(v_out, V_OUT_CREDIT)
                dve.wait_ge(weights_in, 16 * N_LOADS)
                dve.tensor_copy(win[:, 0, :, :], win32[:, :, :]).then_inc(weights_set, 1)
                dve.tensor_copy(sel[:, :, :], sel32[:, :, :]).then_inc(weights_set, 1)
                dve.wait_ge(weights_set, 1)
                dve.tensor_tensor(win[:, 1, :, :], win32[:, :, :], win[:, 0, :, :].bitcast(F32), ALU.subtract)\
                   .then_inc(weights_set, 1)

                def split_w_mm():
                    dve.wait_ge(w_mm_in, 16)
                    dve.tensor_copy(w_mm[:, 0, :, :], stage[:, :, :]).then_inc(weights_set, 1)
                    dve.wait_ge(weights_set, 4)
                    dve.tensor_tensor(w_mm[:, 1, :, :], stage[:, :, :], w_mm[:, 0, :, :].bitcast(F32), ALU.subtract)\
                       .then_inc(weights_set, 1)
                    dve.wait_ge(weights_set, 5)

                def statistics(i, c, n):
                    g, half, slot = at("stats", i, c)
                    base = NORM_TICKS * n

                    def tick(m):
                        dve.wait_ge(ticks, g * (norms * NORM_TICKS) + (base + m))
                    if not first:
                        dve.wait_ge(t_free, g * len(t_uses) + (T_BANKS + GT))
                    elif n == 0:
                        dve.wait_ge(x_in[slot], half * 16 + 16)
                    else:
                        wait_f_taken(dve, g, ("ffn", GT - 1))
                    def aggregate(j):
                        dve.bn_aggr(mean_var[:, j, :], stats[:, j, :]).then_inc(ticks, 1)

                    def add_eps(j):
                        dve.tensor_scalar(var_eps[:, j:j + 1], mean_var[:, j, 1:2], EPS, None, ALU.add)\
                           .then_inc(ticks, 1)

                    for j in range(GT):
                        if j >= 2:
                            tick(j - 1)
                        dve.bn_stats(stats[:, j, :], x_sb[:, slot, j, :]).then_inc(ticks, 1)
                        if j >= 2:
                            aggregate(j - 2)
                    tick(GT)
                    add_eps(0)
                    aggregate(2)
                    tick(GT + 2)
                    add_eps(1)
                    aggregate(3)
                    tick(GT + 4)
                    add_eps(2)
                    tick(GT + 6)
                    add_eps(3)

                def norm(i, c, n):
                    g, _, slot = at("norm", i, c)
                    base = NORM_TICKS * n + STAT_TICKS

                    def tick(m):
                        dve.wait_ge(ticks, g * (norms * NORM_TICKS) + (base + m))
                    dve.wait_ge(std_done, g * norms + (n + 1))
                    dve.reciprocal(rstd[:, 0, :], std[:, :]).then_inc(ticks, 1)
                    tick(1)
                    dve.tensor_tensor(rstd[:, 1, :], rstd[:, 0, :], rstd[:, 0, :], ALU.mult).then_inc(ticks, 1)
                    tick(2)
                    dve.tensor_tensor(rstd[:, 2, :], rstd[:, 1, :], var_eps[:, :], ALU.mult).then_inc(ticks, 1)
                    tick(3)
                    dve.tensor_scalar(rstd[:, 1, :], rstd[:, 2, :], -0.5, 1.5, ALU.mult, ALU.add).then_inc(ticks, 1)
                    tick(4)
                    dve.tensor_tensor(rstd[:, 3, :], rstd[:, 0, :], rstd[:, 1, :], ALU.mult).then_inc(ticks, 1)
                    tick(5)
                    for j in range(GT):
                        dve.tensor_scalar(xn[:, j, :], x_sb[:, slot, j, :], mean_var[:, j, 0:1], rstd[:, 3, j:j + 1],
                                          ALU.subtract, ALU.mult).then_inc(xn_done, 1)

                def turn(i, c, n, kc):
                    g, _, _ = at("turn", i, c)
                    use = t_uses.index(("turn", n, kc))
                    dve.wait_ge(t_first, g * (norms * KC) + (KC * n + kc + 1))
                    dve.tensor_tensor(xt[:, n, 1, kc, :], ps_t[:, use % 2, :], xt[:, n, 0, kc, :].bitcast(F32),
                                      ALU.subtract).then_inc(t_free, 1)

                def proj(i, c, j):
                    g, _, slot = at("proj", i, c)
                    use = t_uses.index(("proj", j))
                    dve.wait_ge(t_done, g * len(t_uses) + (T_DONE_CREDIT + use + 1))
                    dve.wait_ge(x_biased, g * GT + (j + 1))
                    dve.tensor_tensor(x_sb[:, slot, j, :], ps_t[:, use % 2, :], x_sb[:, slot, j, :], ALU.add)\
                       .then_inc(t_free, 1)

                def inputs(i, c):
                    g, _, _ = at("s", i, c)
                    use = f_uses.index(("s",))
                    dve.wait_ge(s_first, g + 1)
                    dve.scalar_tensor_tensor(out=s_parts[M:P, :], in0=ps_f[M:P, use % 2, :], scalar=b_in[M:P, 0:1],
                                             in1=s_parts[M:P, :].bitcast(F32), op0=ALU.add, op1=ALU.subtract)\
                       .then_inc(f_free["dve"], 1)

                def ffn(i, c, j):
                    g, _, slot = at("ffn", i, c)
                    use = f_uses.index(("ffn", j))
                    dve.wait_ge(f_done, g * n_f + (F_DONE_CREDIT + use + 1))
                    dve.scalar_tensor_tensor(out=x_sb[:, slot, j, :], in0=ps_f[:, use % 2, :], scalar=0.5,
                                             in1=x_sb[:, slot, j, :], op0=ALU.mult, op1=ALU.add)\
                       .then_inc(f_free["dve"], 1)

                def project(i, c, j, n):
                    g, _, _ = at("qkv", i, c)
                    use = q_uses.index(("qkv", j, n))
                    if use == 2:
                        dve.wait_ge(v_out, g * 16 + V_OUT_CREDIT)
                    dve.wait_ge(q_done, g * len(q_uses) + (Q_DONE_CREDIT + use + 1))
                    dve.tensor_tensor(qkv[:, j, D * n:D * n + D], ps_q[:, use % 2, :], bias[:, D * n:D * n + D],
                                      ALU.add).then_inc(q_free, 1)

                def rotate(i, c, j):
                    g, _, _ = at("rope", i, c)
                    dve.wait_ge(rope_mul, g * (4 * GT) + 4 * (j + 1))
                    dve.wait_ge(r_done, g * HALVES + (R_DONE_CREDIT + 2 * (j - TURNED_SLOTS + 1)))
                    dve.tensor_tensor(turned_in[:, j % TURNED_SLOTS, :], products[:, 0, :], products[:, 1, :], ALU.add)\
                       .then_inc(rope_done, 1)

                def turn_heads(i, c, h):
                    g, _, _ = at("turn_qk" if h < LATE else "turn_late", i, c)
                    parts = qk_parts[:, h % PARTS_SLOTS, :, :]
                    dve.wait_ge(r_first, g * HALVES + (h + 1))
                    dve.tensor_tensor(parts[:, 1, :], ps_r[:, h % 2, :], parts[:, 0, :].bitcast(F32), ALU.subtract)\
                       .then_inc(r_free, 1)

                do = {"stats": statistics, "norm": norm, "turn": turn, "proj": proj, "s": inputs,
                      "ffn": ffn, "qkv": project, "rope": rotate, "turn_qk": turn_heads,
                      "turn_late": turn_heads}

                def step(i, c):
                    if c == low + 1:
                        split_w_mm()
                    for kind, *x in order:
                        if kind in do and at(kind, i, c):
                            do[kind](i, c, *x)

                schedule(dve, step)


N_IT = B * NHG
M_BANKS = 3
ST_BANKS = 3
PT_SLOTS = 4
QUAD = 4
SUM_SLOTS = 2
PACE = 1.0
FIRST_TOPS = 2
SUM_LAG = 3
Q_ROWS = 3 * DH + 2


def main_steps():
    return [(g, j) for g in reversed(range(GB)) for j in range(GT * (g + 1))]


def off_diagonal(k):
    g, j = main_steps()[k]
    return j < GT * g


def quads():
    return [k for k, (g, j) in enumerate(main_steps()) if j < GT * g and j % QUAD == 0]


def adds_through(k):
    return sum((QUAD - 1) if k >= first + QUAD - 1 else max(1, k - first) for first in quads() if k >= first)


def max_steps():
    out, due = [], []
    for h in range(HG):
        for g in range(GB):
            for r in range(GT):
                for c in range(g + 1):
                    out.append(("chunk", h, g, r, c))
                    if due and len(out) >= due[0][0]:
                        out.append(due.pop(0)[1])
            due.append((len(out) + 8, ("rows", h, g)))
    return out + [d[1] for d in due]


def merged_steps(with_max=True):
    main, tops = main_steps(), max_steps() if with_max else []
    small = []
    for k in range(len(main) + 1):
        if k < len(main):
            small += [("st", k, h) for h in range(HG)]
        if k > 0:
            small += [("pv", k - 1)]
            small += [("sum", first) for first in quads() if first + QUAD - 1 + SUM_LAG == k - 1]
            if not off_diagonal(k - 1):
                small += [("den", k - 1)]

    def tensor_time(step):
        g, j = main[step[1]]
        whole = {"st": 0.22, "pv": 0.92, "den": 0.92, "sum": 0.92}[step[0]]
        return whole * (GT - max(0, j - GT * g)) / GT

    def vector_time(step):
        if step[0] == "rows":
            return 0.0
        _, _, g, r, c = step
        width = (r + 1) * P if c == g else GTOK
        return (0.1 + width / 900.0) + (0.25 if r == GT - 1 and c == g else 0.0)

    reciprocals = 3.3
    whole = sum(tensor_time(x) for x in small if x[1] >= FIRST_TOPS)
    in_all = sum(vector_time(x) for x in tops) + reciprocals * (GB - 1)
    out, done, used, now, ends = [], 0.0, 0.0, 0.0, [0.0] * M_BANKS
    for x in small:
        out.append(x)
        now += tensor_time(x)
        done += tensor_time(x) if x[1] >= FIRST_TOPS else 0.0
        while tops and used < PACE * in_all * done / whole and ends[-M_BANKS] <= now:
            step = tops.pop(0)
            now += 0.22
            used += vector_time(step)
            ends.append(max(ends[-1], now) + vector_time(step))
            out.append(step)
        if x[0] == "den" and main[x[1]][1] == GT * (main[x[1]][0] + 1) - 1:
            used += reciprocals
    return out + tops


def attention(nc, qk_t, v_all, yt_all, ident_in, masks_in):
    main, tops = main_steps(), max_steps()
    n_main, n_tops, n_rows = len(main), len(tops), HG * GB
    both, main_only = merged_steps(), merged_steps(False)
    top_at = {s: i for i, s in enumerate(tops)}
    rows_order = [s for s in tops if s[0] == "rows"]
    unit_at = {s[1:]: i for i, s in enumerate(rows_order)}
    nth_of_kind = [sum(x[0] == s[0] for x in tops[:i + 1]) for i, s in enumerate(tops)]
    n_chunks = n_tops - n_rows
    groups = list(reversed(range(GB)))
    firsts = quads()
    n_adds = len(firsts) * (QUAD - 1)

    def last_use(n, banks, uses):
        return n - banks if n >= banks else max(m for m in range(uses) if m % banks == n % banks) - uses

    n_st = HG * n_main
    den_steps = {g: [x for x in both if x[0] in ("sum", "den") and main[x[1]][0] == g] for g in groups}

    with ExitStack() as ctx:
        def sb(name, shape, dt=F32):
            return ctx.enter_context(nc.sbuf_tensor(name, shape, dt))

        def psum(name, shape):
            return ctx.enter_context(nc.psum_tensor(name, shape, F32))

        def sem(name):
            return ctx.enter_context(nc.semaphore(name))

        ident = sb("a_ident", [P, P])
        masks32 = sb("a_masks32", [P, 2, P])
        ident_bf = sb("a_ident_bf", [P, P], BF16)
        masks_bf = sb("a_masks_bf", [P, 2, P], BF16)
        ones = sb("a_ones", [P, DH])
        q_sb = sb("q_sb", [Q_ROWS, 2, HG, S], F32R)
        k_sb = sb("k_sb", [Q_ROWS, 2, HG, S], F32R)
        v_sb = sb("v_sb", [P, 2, S // P, P])
        probs = sb("probs", [P, PT_SLOTS, HG, GTOK])
        sums = sb("sums", [P, SUM_SLOTS, HG, GTOK])
        y_den = sb("y_den", [P, 2, 2, GTOK])
        chunk_max = sb("chunk_max", [P, 2, GT, GB])
        neg_max = sb("neg_max", [P, 2, GT])
        neg_parts = sb("neg_parts", [P, 2, GT, 2])

        ps_max = psum("ps_max", [P, M_BANKS, GTOK])
        ps_st = psum("ps_st", [P, ST_BANKS, GTOK])
        ps_y = psum("ps_y", [P, GTOK])
        ps_den = psum("ps_den", [P, GTOK])

        consts_in = sem("a_consts_in")
        consts_set = sem("a_consts_set")
        pool_done = sem("a_pool_done")
        qk_in = [[sem("qk_in%d_%d" % (a, g)) for g in range(GB)] for a in range(2)]
        v_in = [sem("v_in0"), sem("v_in1")]
        y_out = [sem("y_out0"), sem("y_out1")]
        scored = sem("scored")
        max_free = sem("max_free")
        rows_taken = sem("rows_taken")
        tops_done = sem("tops_done")
        rows_ready = sem("rows_ready")
        st_done = sem("st_done")
        exp_done = sem("exp_done")
        pv_done = sem("pv_done")
        y_taken = sem("y_taken")
        den_done = sem("den_done")
        y_done = sem("y_done")
        adds_done = sem("adds_done")
        sums_used = sem("sums_used")
        Y_CREDIT, Y_OUT_CREDIT = 1, 1

        with nc.Block() as block:

            @block.sync
            def _(sp):
                sp.dma_start(ident[:, :], ident_in).then_inc(consts_in, 16)
                sp.dma_start(masks32[:, :, :], masks_in).then_inc(consts_in, 16)

                def load_qk(b, hg, a, g):
                    for tile, half, parts in ((k_sb, NHG, (0, 1, 0)), (q_sb, 0, (0, 0, 1))):
                        for n, part in enumerate(parts):
                            src = qk_t[hg + half, part, :, bass.ds(b * S + g * GTOK, GTOK)]
                            sp.dma_start(tile[DH * n:DH * n + DH, a, :, g * GTOK:g * GTOK + GTOK].bitcast(F32),
                                         src.rearrange("(h d) s -> d h s", h=HG)).then_inc(qk_in[a][g], 16)

                def load_v(b, hg, a, g):
                    src = v_all[bass.ds(b * S + g * GTOK, GTOK), hg * P:hg * P + P]
                    sp.dma_start(v_sb[:, a, g * GT:g * GT + GT, :], src.rearrange("(j p) c -> p j c", p=P))\
                      .then_inc(v_in[a], 16)

                def store(b, hg, n):
                    sp.wait_ge(y_done, b * (NHG * GB) + (hg * GB + n + 1))
                    dst = yt_all[bass.ds(b * GB + groups[n], 1), hg, :, :]
                    sp.dma_start(dst.rearrange("o p s -> (o p) s"), y_den[:, n % 2, 0, :]).then_inc(y_out[n % 2], 16)

                def batch(b, last):
                    for hg in range(NHG):
                        for n, g in enumerate(groups):
                            if 0 < n < GB - 1:
                                store(b, hg, n - 1)
                            if hg + 2 < NHG or not last:
                                nb, nhg = b + (hg + 2) // NHG, (hg + 2) % NHG
                                done = sum(GT * (x + 1) for x in groups[:n + 1])
                                sp.wait_ge(st_done, b * (NHG * n_st) + (hg * n_st + HG * done))
                                load_qk(nb, nhg, hg % 2, g)
                                sp.wait_ge(pv_done, b * (NHG * n_main) + (hg * n_main + PT_SLOTS + done))
                                load_v(nb, nhg, hg % 2, g)
                        for n in range(GB - 2, GB):
                            store(b, hg, n)

                for n in range(2):
                    for g in range(GB):
                        load_qk(0, n, n, g)
                    for g in range(GB):
                        load_v(0, n, n, g)
                with sp.Fori(0, B - 1) as b:
                    batch(b, False)
                batch(B - 1, True)
                for n in range(2):
                    sp.wait_ge(y_out[n], 16 * (Y_OUT_CREDIT + N_IT * GB // 2))

            @block.gpsimd
            def _(pool):
                for a in range(2):
                    pool.memset(k_sb[3 * DH:Q_ROWS, a, :, :].bitcast(F32), 1.0).then_inc(pool_done, 1)
                    pool.wait_ge(pool_done, a + 1)
                pool.memset(ones[:, :], 1.0).then_inc(pool_done, 1)
                pool.sem_inc(y_out[0], 16 * Y_OUT_CREDIT)
                pool.sem_inc(y_out[1], 16 * Y_OUT_CREDIT)

                def add_quad(it, u):
                    out = sums[:, u % SUM_SLOTS, :, :]
                    pool.wait_ge(sums_used, it * len(firsts) + (u + 1))
                    for n in range(1, QUAD):
                        k = firsts[u] + n
                        pool.wait_ge(exp_done, it * n_st + (ST_BANKS + HG * k + HG))
                        if n > 1:
                            pool.wait_ge(adds_done, it * n_adds + ((QUAD - 1) * u + n - 1))
                        before = probs[:, (k - 1) % PT_SLOTS, :, :] if n == 1 else out
                        pool.tensor_tensor(out, before, probs[:, k % PT_SLOTS, :, :], ALU.add).then_inc(adds_done, 1)

                def divide(it, n):
                    pool.wait_ge(den_done, it * (GB * GT) + GT * (n + 1))
                    y = y_den[:, n % 2, 0, :]
                    pool.tensor_tensor(y, y, y_den[:, n % 2, 1, :], ALU.mult).then_inc(y_done, 1)

                with pool.Fori(0, N_IT) as it:
                    for n, g in enumerate(groups):
                        for u, first in enumerate(firsts):
                            if main[first][0] == g:
                                add_quad(it, u)
                        if n > 0:
                            divide(it, n - 1)
                    divide(it, GB - 1)

            @block.tensor
            def _(pe):
                pe.sem_inc(pv_done, PT_SLOTS)
                pe.sem_inc(sums_used, SUM_SLOTS)
                pe.wait_ge(consts_in, 32)
                pe.wait_ge(consts_set, 2)
                pe.wait_ge(pool_done, 3)

                def wait_bank(it, n):
                    m = last_use(n, M_BANKS, n_tops)
                    taken, per = (max_free, n_chunks) if tops[m][0] == "chunk" else (rows_taken, n_rows)
                    pe.wait_ge(taken, it * per + (per + M_BANKS + nth_of_kind[m] - (per if m < 0 else 0)))

                def chunk(it, loads, a, step):
                    _, h, g, r, c = step
                    n = top_at[step]
                    if h == 0 and r == 0 and c == 0:
                        pe.wait_ge(qk_in[a][g], loads * (6 * 16))
                    wait_bank(it, n)
                    diagonal = c == g
                    width = (r + 1) * P if diagonal else GTOK
                    row = GTOK * g + P * r
                    mm = pe.matmul(ps_max[:, n % M_BANKS, 0:width], q_sb[0:3 * DH, a, h, row:row + P],
                                   k_sb[0:3 * DH, a, h, GTOK * c:GTOK * c + width], start=True, stop=not diagonal)
                    if diagonal:
                        mm = pe.matmul(ps_max[:, n % M_BANKS, P * r:P * r + P], ident_bf[:, :], masks_bf[:, 0, :],
                                       start=False, stop=True)
                    mm.then_inc(scored, 1)

                def rows(it, step):
                    n, u = top_at[step], unit_at[step[1:]]
                    wait_bank(it, n)
                    pe.wait_ge(rows_ready, it * n_rows + (n_rows + u + 1))
                    for r in range(GT):
                        mm = pe.transpose(ps_max[0:2, n % M_BANKS, P * r:P * r + P], neg_parts[:, u % 2, r, :],
                                          ident[:, :])
                    mm.then_inc(scored, 1)

                def scores_t(it, a, k, h):
                    g, j = main[k]
                    n = HG * k + h
                    if n == 0:
                        pe.wait_ge(rows_taken, it * n_rows + (M_BANKS + n_rows))
                    pe.wait_ge(exp_done, it * n_st + (ST_BANKS + 1 + last_use(n, ST_BANKS, n_st)))
                    c0 = P * max(0, j - GT * g)
                    out = ps_st[:, n % ST_BANKS, :]
                    diagonal = j >= GT * g
                    mm = pe.matmul(out[:, c0:GTOK], k_sb[:, a, h, P * j:P * j + P],
                                   q_sb[:, a, h, GTOK * g + c0:GTOK * g + GTOK], start=True, stop=not diagonal)
                    if diagonal:
                        mm = pe.matmul(out[:, c0:c0 + P], ident_bf[:, :], masks_bf[:, 1, :], start=False, stop=True)
                    mm.then_inc(st_done, 1)

                def products(it, loads, a, k):
                    g, j = main[k]
                    if k == 0:
                        pe.wait_ge(v_in[a], loads * (GB * 16))
                    if j == 0:
                        pe.wait_ge(y_taken, it * GB + (Y_CREDIT + groups.index(g)))
                    pe.wait_ge(exp_done, it * n_st + (ST_BANKS + HG * k + HG))
                    c0 = P * max(0, j - GT * g)
                    for h in range(HG):
                        rows = slice(DH * h, DH * h + DH)
                        mm = pe.matmul(ps_y[rows, c0:GTOK], v_sb[:, a, j, rows], probs[:, k % PT_SLOTS, h, c0:GTOK],
                                       start=j == 0, stop=j == GT * (g + 1) - 1)
                    if off_diagonal(k):
                        mm.then_inc(pv_done, 1)

                def denominators(it, step):
                    kind, k = step
                    g, j = main[k]
                    c0 = P * max(0, j - GT * g)
                    if kind == "sum":
                        u = firsts.index(k)
                        pe.wait_ge(adds_done, it * n_adds + (QUAD - 1) * (u + 1))
                        src = sums[:, u % SUM_SLOTS, :, :]
                    else:
                        src = probs[:, k % PT_SLOTS, :, :]
                    for h in range(HG):
                        mm = pe.matmul(ps_den[DH * h:DH * h + DH, c0:GTOK], ones[:, :], src[:, h, c0:GTOK],
                                       start=step == den_steps[g][0], stop=step == den_steps[g][-1])
                    mm.then_inc(sums_used if kind == "sum" else pv_done, 1)

                def iteration(it, loads, a, ahead):
                    for step in both if ahead is not None else main_only:
                        if step[0] == "st":
                            scores_t(it, a, step[1], step[2])
                        elif step[0] == "pv":
                            products(it, loads, a, step[1])
                        elif step[0] in ("sum", "den"):
                            denominators(it, step)
                        elif step[0] == "chunk":
                            chunk(it, ahead, 1 - a, step)
                        else:
                            rows(it, step)

                for step in tops:
                    if step[0] == "chunk":
                        chunk(-1, 1, 0, step)
                    else:
                        rows(-1, step)
                with pe.Fori(0, N_IT // 2 - 1) as i:
                    iteration(i * 2, i + 1, 0, i + 1)
                    iteration(i * 2 + 1, i + 1, 1, i + 2)
                iteration(N_IT - 2, N_IT // 2, 0, N_IT // 2)
                iteration(N_IT - 1, N_IT // 2, 1, None)

            @block.scalar
            def _(act):
                act.sem_inc(exp_done, ST_BANKS)
                act.sem_inc(y_taken, Y_CREDIT)
                act.sem_inc(rows_taken, M_BANKS)

                def take_rows(im, a, step):
                    _, h, g = step
                    n = top_at[step]
                    act.wait_ge(scored, im * n_tops + (n + 1))
                    act.copy(q_sb[3 * DH:Q_ROWS, a, h, GTOK * g:GTOK * g + GTOK], ps_max[0:2, n % M_BANKS, :])\
                       .then_inc(rows_taken, 1)

                def exponentials(it, k, h):
                    g, j = main[k]
                    c0 = P * max(0, j - GT * g)
                    if h == 0:
                        act.wait_ge(pv_done, it * n_main + (k + 1))
                        before = k - PT_SLOTS
                        if before >= 0 and off_diagonal(before):
                            act.wait_ge(adds_done, it * n_adds + adds_through(before))
                    n = HG * k + h
                    act.wait_ge(st_done, it * n_st + (n + 1))
                    act.activation(probs[:, k % PT_SLOTS, h, c0:GTOK], ps_st[:, n % ST_BANKS, c0:GTOK], ACT.Exp)\
                       .then_inc(exp_done, 1)

                def take_y(it, n):
                    done = sum(GT * (x + 1) for x in groups[:n + 1])
                    act.wait_ge(pv_done, it * n_main + (PT_SLOTS + done))
                    act.wait_ge(y_out[n % 2], it * (16 * GB // 2) + 16 * (n // 2 + 1))
                    act.copy(y_den[:, n % 2, 0, :], ps_y[:, :])
                    act.copy(y_den[:, n % 2, 1, :], ps_den[:, :]).then_inc(y_taken, 1)

                def iteration(it, a, ahead):
                    for step in both if ahead else main_only:
                        if step[0] == "rows":
                            take_rows(it + 1, 1 - a, step)
                        elif step[0] == "st":
                            _, k, h = step
                            exponentials(it, k, h)
                            g, j = main[k]
                            if h == HG - 1 and j == 0 and k > 0:
                                take_y(it, groups.index(g) - 1)
                    take_y(it, GB - 1)

                for step in rows_order:
                    take_rows(0, 0, step)
                with act.Fori(0, N_IT // 2 - 1) as i:
                    iteration(i * 2, 0, True)
                    iteration(i * 2 + 1, 1, True)
                iteration(N_IT - 2, 0, True)
                iteration(N_IT - 1, 1, False)

            @block.vector
            def _(dve):
                dve.sem_inc(max_free, M_BANKS)
                dve.wait_ge(consts_in, 32)
                dve.tensor_copy(ident_bf[:, :], ident[:, :]).then_inc(consts_set, 1)
                dve.tensor_copy(masks_bf[:, :, :], masks32[:, :, :]).then_inc(consts_set, 1)

                def take_max(im, step):
                    _, h, g, r, c = step
                    n, u = top_at[step], unit_at[h, g]
                    width = (r + 1) * P if c == g else GTOK
                    dve.wait_ge(scored, im * n_tops + (n + 1))
                    dve.tensor_reduce(chunk_max[:, u % 2, r, c:c + 1], ps_max[:, n % M_BANKS, 0:width], AX_X,
                                      ALU.max).then_inc(max_free, 1)

                def negate(im, u, h, g):
                    n = top_at["chunk", h, g, GT - 1, g]
                    dve.wait_ge(max_free, im * n_chunks + (M_BANKS + nth_of_kind[n]))
                    dve.tensor_reduce(neg_max[:, u % 2, :], chunk_max[:, u % 2, :, 0:g + 1], AX_X, ALU.max,
                                      negate=True).then_inc(tops_done, 1)

                def first_part(im, u, h, g):
                    dve.wait_ge(tops_done, im * (2 * n_rows) + (2 * u + 1))
                    dve.tensor_copy(neg_parts[:, u % 2, :, 0].bitcast(F32R), neg_max[:, u % 2, :])\
                       .then_inc(tops_done, 1)

                def second_part(im, u, h, g):
                    dve.wait_ge(tops_done, im * (2 * n_rows) + (2 * u + 2))
                    dve.tensor_tensor(neg_parts[:, u % 2, :, 1].bitcast(F32R), neg_max[:, u % 2, :],
                                      neg_parts[:, u % 2, :, 0], ALU.subtract).then_inc(rows_ready, 1)

                def reciprocal(it, n, r):
                    if r == 0:
                        dve.wait_ge(y_taken, it * GB + (Y_CREDIT + n + 1))
                    den = y_den[:, n % 2, 1, P * r:P * r + P]
                    dve.reciprocal(den, den).then_inc(den_done, 1)

                def iteration(it, im, steps):
                    small, quarters = [], []
                    for step in steps:
                        if step[0] == "chunk":
                            take_max(im, step)
                            if small:
                                what, *x = small.pop(0)
                                what(im, *x)
                            elif quarters:
                                reciprocal(it, *quarters.pop(0))
                            _, h, g, r, c = step
                            if r == GT - 1 and c == g:
                                small += [(what, unit_at[h, g], h, g) for what in (negate, first_part, second_part)]
                        elif step[0] == "rows":
                            while any(x[2:] == step[1:] for x in small):
                                what, *x = small.pop(0)
                                what(im, *x)
                        elif step[0] == "den":
                            g, j = main[step[1]]
                            if j == GT * (g + 1) - 1:
                                quarters += [(groups.index(g), r) for r in range(GT)]
                    for x in quarters:
                        reciprocal(it, *x)

                iteration(None, 0, tops)
                with dve.Fori(0, N_IT // 2 - 1) as i:
                    iteration(i * 2, i * 2 + 1, both)
                    iteration(i * 2 + 1, i * 2 + 2, both)
                iteration(N_IT - 2, N_IT - 1, both)
                iteration(N_IT - 1, None, main_only)


def macaron_block(nc, x, w, out):
    x_mid = nc.dram_tensor("x_mid", (TOK, D), F32).ap()
    qk_t = nc.dram_tensor("qk_t", (2 * NHG, 2, P, TOK), F32).ap()
    v_all = nc.dram_tensor("v_all", (TOK, D), F32).ap()
    yt_all = nc.dram_tensor("yt_all", (NG, NHG, P, GTOK), F32).ap()
    dense(nc, True, w, x, x_mid, None, qk_t, v_all)
    attention(nc, qk_t, v_all, yt_all, w["ident"], w["masks"])
    dense(nc, False, w, x_mid, out, yt_all, None, None)


def constants():
    c = {"ident": np.eye(P, dtype=np.float32)}
    lower = np.tril(np.ones((P, P), bool))
    c["masks"] = np.stack([np.where(lower, 0.0, MASK), np.where(lower.T, 0.0, MASK)], 1).astype(np.float32)
    unit = np.arange(NE * P) // INNER
    c["sel"] = (np.arange(P)[:, None] % M == unit[None, :]).astype(np.float32).reshape(P, NE, P)
    angles = np.arange(S, dtype=np.float32)[:, None] / np.float32(10000.0) ** (
        np.arange(0, DH, 2, dtype=np.float32) / np.float32(DH))
    cos, sin = np.cos(angles), np.sin(angles)
    own = np.concatenate([cos, sin], 1)
    other = np.concatenate([-(1 - cos), 1 - sin], 1)
    both = np.stack([own, other], 1)
    table = np.stack([both * np.float32(DH ** -0.5), both], 1).astype(np.float32)
    c["rope"] = np.tile(table.reshape(S, 4 * DH), (B, 1))
    return c


def kernel(L0_attn_x, L0_attn_Wqkv, L0_attn_bqkv, L0_attn_Wproj, L0_attn_bproj, L0_ffn_Win, L0_ffn_bin_, L0_ffn_W1,
           L0_ffn_b1, L0_ffn_W2, L0_ffn_b2, L0_ffn_Wout, L0_ffn_bout):
    import concourse.bacc as bacc
    from concourse.bass_utils import run_bass_kernel_spmd

    def heads(a):
        a = np.asarray(a).reshape((H, 3, DH) + np.asarray(a).shape[1:])
        qk = a[:, :2].reshape((H, 2, DH // 2, 2) + a.shape[3:])
        qk = np.moveaxis(qk, 3, 2).reshape((H, 2, DH) + a.shape[3:])
        return np.concatenate([qk, a[:, 2:]], 1).swapaxes(0, 1).reshape((3 * D,) + a.shape[3:])

    place = [DH * (m // 8 % 4) + 8 * (m // 32) + m % 8 for m in range(M)]
    w2 = np.zeros((P, NE, DH), np.float32)
    b2 = np.zeros((P, 1), np.float32)
    w_out = np.zeros((P, D), np.float32)
    for m in range(M):
        row = INNER * (m % 8)
        w2[row:row + INNER, m // 8, place[m] % DH] = np.asarray(L0_ffn_W2)[m]
        b2[place[m], 0] = np.asarray(L0_ffn_b2)[m]
        w_out[place[m]] = np.asarray(L0_ffn_Wout)[m]
    b2[DH // 2, 0] = 1.0
    w_out[DH // 2] = np.asarray(L0_ffn_bout)
    arrays = {
        "x": np.asarray(L0_attn_x).reshape(TOK, D),
        "w_qkv": heads(L0_attn_Wqkv).T, "b_qkv": heads(L0_attn_bqkv),
        "w_proj": np.asarray(L0_attn_Wproj).T, "b_proj": np.asarray(L0_attn_bproj),
        "w_in": np.asarray(L0_ffn_Win),
        "b_in": np.concatenate([np.asarray(L0_ffn_bin_)] * 2).reshape(P, 1),
        "w1": np.asarray(L0_ffn_W1).reshape(NE, P).T, "b1": np.asarray(L0_ffn_b1).reshape(NE, P).T,
        "w2": w2, "b2": b2, "w_out": w_out, **constants(),
    }
    arrays = {k: np.ascontiguousarray(v) for k, v in arrays.items()}

    nc = bacc.Bacc("TRN2", target_bir_lowering=False, num_devices=1)
    aps = {k: nc.dram_tensor("in_" + k, v.shape, F32, kind="ExternalInput").ap() for k, v in arrays.items()}
    out = nc.dram_tensor("out", (TOK, D), F32, kind="ExternalOutput").ap()
    macaron_block(nc, aps["x"], aps, out)
    result = run_bass_kernel_spmd(nc, [{"in_" + k: v for k, v in arrays.items()}], core_ids=[0])
    return result.results[0]["out"].reshape(B, S, D)
```
